# Optimizing a Trainium2 kernel written in Bass

```python
import numpy as np
import jax
import jax.numpy as jnp

def _softmax(x, axis=-1):
    return jax.nn.softmax(x, axis=axis)

def _gelu(x):
    return jax.nn.gelu(x, approximate=True)

def _silu(x):
    return jax.nn.silu(x)

def _sigmoid(x):
    return jax.nn.sigmoid(x)

def _layernorm(x, axis=-1, eps=1e-05):
    m = jnp.mean(x, axis=axis, keepdims=True)
    v = jnp.var(x, axis=axis, keepdims=True)
    return (x - m) / jnp.sqrt(v + eps)

def _scatter_add(tgt, idx, src, axis=0):
    return tgt.at[idx].add(src)

def _segment_sum(src, seg, n):
    return jax.ops.segment_sum(src, seg, n)
kernel_name = 'mk_hybrid_d1_jaxref_r4_5c62de'

def setup_inputs(seed: int=0):
    np.random.seed(seed)
    _w = jnp.asarray

    def _L0_attn_a_setup():
        import jax, jax.numpy as jnp
        import numpy as np
        import math
        D = 512
        K = 64
        NUM_HEADS = 32
        HEAD_DIM = K // NUM_HEADS
        SPARSITY = 0.1
        LN_EPS = 1e-05
        key = jax.random.key(seed)
        ks = jax.random.split(key, 12)
        B, S = (1, 256)
        sc = 0.02
        inp = {'x': jax.random.normal(ks[0], (B, S, D), dtype=jnp.float32), 'gamma': jnp.ones((D,), jnp.float32), 'beta': jnp.zeros((D,), jnp.float32), 'W1': jax.random.normal(ks[1], (128, D), jnp.float32) * sc, 'b1': jnp.zeros((128,), jnp.float32), 'W2': jax.random.normal(ks[2], (64, 128), jnp.float32) * sc, 'b2': jnp.zeros((64,), jnp.float32), 'W3': jax.random.normal(ks[3], (1, 64), jnp.float32) * sc, 'b3': jnp.zeros((1,), jnp.float32), 'Wqkv': jax.random.normal(ks[4], (3 * K, D), jnp.float32) * sc, 'bqkv': jnp.zeros((3 * K,), jnp.float32), 'Wout': jax.random.normal(ks[5], (D, K), jnp.float32) * sc, 'bout': jnp.zeros((D,), jnp.float32)}
        return inp
    _L0_attn_a_in = _L0_attn_a_setup()

    def _L0_attn_b_setup():
        import jax, jax.numpy as jnp
        import numpy as np
        import math
        N_HEAD = 16
        LAYER = 1
        LAMBDA_INIT = 0.8 - 0.6 * math.exp(-0.3 * (LAYER - 1))
        key = jax.random.key(seed)
        ks = jax.random.split(key, 7)
        B, T, E = (2, 512, 512)
        s = 0.02
        return {'x': jax.random.normal(ks[0], (B, T, E), dtype=jnp.float32), 'W_attn': jax.random.normal(ks[1], (E, 3 * E), dtype=jnp.float32) * s, 'W_proj': jax.random.normal(ks[2], (E, E), dtype=jnp.float32) * s, 'lambda_q1': jax.random.normal(ks[3], (E,), dtype=jnp.float32) * 0.1, 'lambda_k1': jax.random.normal(ks[4], (E,), dtype=jnp.float32) * 0.1, 'lambda_q2': jax.random.normal(ks[5], (E,), dtype=jnp.float32) * 0.1, 'lambda_k2': jax.random.normal(ks[6], (E,), dtype=jnp.float32) * 0.1}
    _L0_attn_b_in = _L0_attn_b_setup()

    def _L0_ffn_setup():
        import jax, jax.numpy as jnp
        import numpy as np
        HIDDEN = 512
        INTER = 2048
        BATCH, LOCAL_SEQ = (2, 1024)
        key = jax.random.key(seed)
        k1, k2, k3 = jax.random.split(key, 3)
        h_shard = jax.random.normal(k1, (BATCH, LOCAL_SEQ, HIDDEN), dtype=jnp.float32)
        w_gate_up = jax.random.normal(k2, (2 * INTER, HIDDEN), dtype=jnp.float32) * 0.02
        w_down = jax.random.normal(k3, (HIDDEN, INTER), dtype=jnp.float32) * 0.02
        return {'h_shard': h_shard, 'w_gate_up': w_gate_up, 'w_down': w_down}
    _L0_ffn_in = _L0_ffn_setup()
    _d = {'L0_attn_a_x': _L0_attn_a_in['x'], 'L0_attn_a_gamma': _L0_attn_a_in['gamma'], 'L0_attn_a_beta': _L0_attn_a_in['beta'], 'L0_attn_a_W1': _L0_attn_a_in['W1'], 'L0_attn_a_b1': _L0_attn_a_in['b1'], 'L0_attn_a_W2': _L0_attn_a_in['W2'], 'L0_attn_a_b2': _L0_attn_a_in['b2'], 'L0_attn_a_W3': _L0_attn_a_in['W3'], 'L0_attn_a_b3': _L0_attn_a_in['b3'], 'L0_attn_a_Wqkv': _L0_attn_a_in['Wqkv'], 'L0_attn_a_bqkv': _L0_attn_a_in['bqkv'], 'L0_attn_a_Wout': _L0_attn_a_in['Wout'], 'L0_attn_a_bout': _L0_attn_a_in['bout'], 'L0_attn_b_W_attn': _L0_attn_b_in['W_attn'], 'L0_attn_b_W_proj': _L0_attn_b_in['W_proj'], 'L0_attn_b_lambda_q1': _L0_attn_b_in['lambda_q1'], 'L0_attn_b_lambda_k1': _L0_attn_b_in['lambda_k1'], 'L0_attn_b_lambda_q2': _L0_attn_b_in['lambda_q2'], 'L0_attn_b_lambda_k2': _L0_attn_b_in['lambda_k2'], 'L0_ffn_w_gate_up': _L0_ffn_in['w_gate_up'], 'L0_ffn_w_down': _L0_ffn_in['w_down']}
    _x0 = _d['L0_attn_a_x']
    _d['L0_attn_a_x'] = jax.random.normal(jax.random.fold_in(jax.random.key(seed), 1), (4, 512, 512), dtype=_x0.dtype)
    del _x0
    return _d

def reference(L0_attn_a_x, L0_attn_a_gamma, L0_attn_a_beta, L0_attn_a_W1, L0_attn_a_b1, L0_attn_a_W2, L0_attn_a_b2, L0_attn_a_W3, L0_attn_a_b3, L0_attn_a_Wqkv, L0_attn_a_bqkv, L0_attn_a_Wout, L0_attn_a_bout, L0_attn_b_W_attn, L0_attn_b_W_proj, L0_attn_b_lambda_q1, L0_attn_b_lambda_k1, L0_attn_b_lambda_q2, L0_attn_b_lambda_k2, L0_ffn_w_gate_up, L0_ffn_w_down):

    def _L0_attn_a_ref(x, gamma, beta, W1, b1, W2, b2, W3, b3, Wqkv, bqkv, Wout, bout):
        import jax, jax.numpy as jnp
        import numpy as np
        import math
        D = 512
        K = 64
        NUM_HEADS = 32
        HEAD_DIM = K // NUM_HEADS
        SPARSITY = 0.1
        LN_EPS = 1e-05
        B, S, d = x.shape
        mu = jnp.mean(x, -1, keepdims=True)
        var = jnp.var(x, -1, keepdims=True)
        xn = (x - mu) * jax.lax.rsqrt(var + LN_EPS) * gamma + beta
        h = jnp.einsum('bsd,fd->bsf', xn, W1)
        pair = jax.nn.relu(h[:, :, None, :] - h[:, None, :, :] + b1)
        pair = jax.nn.relu(jnp.einsum('bijf,gf->bijg', pair, W2) + b2)
        sim = jnp.einsum('bijg,og->bijo', pair, W3)[..., 0] + b3[0]
        diag = jnp.arange(S)
        sim = sim.at[:, diag, diag].set(0.0)
        k_sparse = max(1, int(S * SPARSITY))
        _, top_idx = jax.lax.top_k(sim, k_sparse)
        mask = jnp.full((B, S, S), -jnp.inf, dtype=x.dtype)
        bidx = jnp.arange(B)[:, None, None]
        iidx = jnp.arange(S)[None, :, None]
        mask = mask.at[bidx, iidx, top_idx].set(0.0)
        qkv = jnp.einsum('bsd,ed->bse', xn, Wqkv) + bqkv
        q, k, v = jnp.split(qkv, 3, axis=-1)

        def heads(t):
            return t.reshape(B, S, NUM_HEADS, HEAD_DIM).transpose(0, 2, 1, 3)
        q, k, v = (heads(q), heads(k), heads(v))
        scores = jnp.einsum('bhid,bhjd->bhij', q, k) / math.sqrt(HEAD_DIM)
        scores = scores + mask[:, None, :, :]
        attn = jax.nn.softmax(scores, axis=-1)
        ao = jnp.einsum('bhij,bhjd->bhid', attn, v)
        ao = ao.transpose(0, 2, 1, 3).reshape(B, S, K)
        out = jnp.einsum('bsk,dk->bsd', ao, Wout) + bout
        return x + out

    def _L0_attn_b_ref(x, W_attn, W_proj, lambda_q1, lambda_k1, lambda_q2, lambda_k2):
        import jax, jax.numpy as jnp
        import numpy as np
        import math
        N_HEAD = 16
        LAYER = 1
        LAMBDA_INIT = 0.8 - 0.6 * math.exp(-0.3 * (LAYER - 1))
        B, T, E = x.shape
        C = E // 2
        H = N_HEAD
        hd = E // H // 2
        scale = hd ** (-0.5)
        qkv = x @ W_attn
        q1 = qkv[..., 0 * C:1 * C].reshape(B, T, H, hd)
        k1 = qkv[..., 1 * C:2 * C].reshape(B, T, H, hd)
        q2 = qkv[..., 2 * C:3 * C].reshape(B, T, H, hd)
        k2 = qkv[..., 3 * C:4 * C].reshape(B, T, H, hd)
        v = qkv[..., 4 * C:6 * C].reshape(B, T, H, 2 * hd)
        lam = jnp.exp(jnp.dot(lambda_q1, lambda_k1)) - jnp.exp(jnp.dot(lambda_q2, lambda_k2)) + LAMBDA_INIT
        attn1 = jnp.einsum('bthd,bshd->bhts', q1, k1) * scale
        attn2 = jnp.einsum('bthd,bshd->bhts', q2, k2) * scale
        score = jax.nn.softmax(attn1 - lam * attn2, axis=-1)
        out = jnp.einsum('bhts,bshd->bthd', score, v)
        out = (1.0 - LAMBDA_INIT) * out.reshape(B, T, E)
        return out @ W_proj

    def _L0_ffn_ref(h_shard, w_gate_up, w_down):
        import jax, jax.numpy as jnp
        import numpy as np
        HIDDEN = 512
        INTER = 2048
        BATCH, LOCAL_SEQ = (2, 1024)
        batch, local_seq, hidden = h_shard.shape
        gate_up = jnp.einsum('bsh,oh->bso', h_shard, w_gate_up)
        gate, up = jnp.split(gate_up, 2, axis=-1)
        h = jax.nn.silu(gate) * up
        out = jnp.einsum('bsi,hi->bsh', h, w_down)
        return out
    x = L0_attn_a_x
    x = x + _L0_attn_a_ref(_layernorm(x, axis=-1), L0_attn_a_gamma, L0_attn_a_beta, L0_attn_a_W1, L0_attn_a_b1, L0_attn_a_W2, L0_attn_a_b2, L0_attn_a_W3, L0_attn_a_b3, L0_attn_a_Wqkv, L0_attn_a_bqkv, L0_attn_a_Wout, L0_attn_a_bout)
    x = x + _L0_ffn_ref(_layernorm(x, axis=-1), L0_ffn_w_gate_up, L0_ffn_w_down)
    x = x + _L0_attn_b_ref(_layernorm(x, axis=-1), L0_attn_b_W_attn, L0_attn_b_W_proj, L0_attn_b_lambda_q1, L0_attn_b_lambda_k1, L0_attn_b_lambda_q2, L0_attn_b_lambda_k2)
    x = x + _L0_ffn_ref(_layernorm(x, axis=-1), L0_ffn_w_gate_up, L0_ffn_w_down)
    return x

_drawn_inputs = setup_inputs


def setup_inputs(seed=0):
    import zlib

    import numpy as np

    out = dict(_drawn_inputs(seed))
    spreads = {'L0_attn_a_gamma': (1.0, 0.6),
     'L0_attn_a_beta': (0.0, 0.8),
     'L0_attn_a_b1': (0.0, 0.8),
     'L0_attn_a_b2': (0.0, 0.8),
     'L0_attn_a_bqkv': (0.0, 0.8),
     'L0_attn_a_bout': (0.0, 0.1)}
    factors = {'L0_attn_a_W1': 8.0,
     'L0_attn_a_W2': 8.0,
     'L0_attn_a_W3': 8.0,
     'L0_attn_a_Wqkv': 8.0,
     'L0_attn_a_Wout': 4.904,
     'L0_attn_b_W_attn': 8.0,
     'L0_attn_b_W_proj': 8.0,
     'L0_attn_b_lambda_q1': 8.0,
     'L0_attn_b_lambda_k1': 8.0,
     'L0_attn_b_lambda_q2': 64.0,
     'L0_attn_b_lambda_k2': 8.0}
    for name, (base, spread) in spreads.items():
        noise = np.random.default_rng([zlib.crc32(name.encode()), seed]).standard_normal(out[name].shape)
        drawn = base * np.exp(spread * noise) if base else spread * noise
        out[name] = jnp.asarray(drawn.astype(out[name].dtype))
    for name, factor in factors.items():
        out[name] = (out[name] * factor).astype(out[name].dtype)
    return out
```

```python
from contextlib import ExitStack

import concourse.bass as bass
from concourse import mybir

ALU = mybir.AluOpType
ACT = mybir.ActivationFunctionType
AX = mybir.AxisListType
F32 = mybir.dt.float32
F32R = mybir.dt.float32r
BF16 = mybir.dt.bfloat16

P = 128
B, S, D = 4, 512, 512
NT = S // P
ND = D // P
F1, F2 = 128, 64
TOPK = max(1, int(S * 0.1))
HA, KA = 32, 64
HB, HDB = 16, 16
INTER = 2048
NI = INTER // P
LN_EPS = 1e-5
LAMBDA_INIT = 0.8 - 0.6 * 1.0
MASKED = -1e30
TAKEN = -3e38
SENTINEL = 3e38
NEVAL = -2.9e38
PAD = (-TOPK) % 8
HALVES = 6
STACK = 16 * (HALVES + 1)


class Lane:

    def __init__(self, nc, ctx, engine, name):
        self.nc, self.ctx, self.engine, self.name = nc, ctx, engine, name
        self.waited = {}
        self.last = None

    def phase(self, name):
        self.sem_name = f"{self.name}_{name}"
        self.sem = self.ctx.enter_context(self.nc.semaphore(self.sem_name))
        self.count = 0

    def did(self, instruction):
        self.count += 1
        instruction.then_inc(self.sem, 1)
        self.last = (self.sem_name, self.sem, self.count)
        return self.last

    def after(self, *signals):
        for signal in signals:
            if signal is None:
                continue
            name, sem, value = signal
            if self.waited.get(name, 0) < value:
                self.engine.wait_ge(sem, value)
                self.waited[name] = value


class Transfers:

    def __init__(self, nc, ctx, name):
        self.name, self.sem, self.count = name, ctx.enter_context(nc.semaphore(name)), 0

    def start(self, lane, out, in_):
        self.count += 16
        lane.engine.dma_start(out, in_).then_inc(self.sem, 16)
        return self.all()

    def all(self):
        return (self.name, self.sem, self.count)


class Core:
    pass


def build(nc, d, upto=9):
    with ExitStack() as ctx:
        pe = Lane(nc, ctx, nc.tensor, "pe")
        dve = Lane(nc, ctx, nc.vector, "dve")
        act = Lane(nc, ctx, nc.scalar, "act")
        pool = Lane(nc, ctx, nc.gpsimd, "pool")
        sp = Lane(nc, ctx, nc.sync, "sp")
        lanes = (pe, dve, act, pool, sp)

        def sb(mem, name, shape, dt=F32):
            return mem.enter_context(nc.sbuf_tensor(name, shape, dt))

        def phase(name):
            old = [lane.last for lane in lanes]
            for lane in lanes:
                lane.after(*old)
                lane.phase(name)

        def transfers(name):
            return Transfers(nc, ctx, name)

        ps = ctx.enter_context(nc.psum_tensor("ps", [P, 8, 512], F32))
        x = sb(ctx, "x", [P, B * NT, D])
        ident = sb(ctx, "ident", [P, P])
        ident_bf = sb(ctx, "ident_bf", [P, P], BF16)
        ln_stats = sb(ctx, "ln_stats", [P, NT, 6])
        ln_mv = sb(ctx, "ln_mv", [P, NT, 2])
        ln_var = sb(ctx, "ln_var", [P, NT])
        ln_sd = sb(ctx, "ln_sd", [P, NT])
        ln_r0 = sb(ctx, "ln_r0", [P, NT])
        ln_t = sb(ctx, "ln_t", [P, NT])
        ln_rs = sb(ctx, "ln_rs", [P, NT])

        def layer_norm(src, dst, ready, free=None):
            dve.after(ready)
            for t in range(NT):
                s = dve.did(nc.vector.bn_stats(ln_stats[:, t, :], src(t)))
            dve.after(s)
            for t in range(NT):
                s = dve.did(nc.vector.bn_aggr(ln_mv[:, t, :], ln_stats[:, t, :]))
            dve.after(s)
            s = dve.did(nc.vector.tensor_scalar(ln_var[:, :], ln_mv[:, :, 1], LN_EPS, None, ALU.add))
            act.after(s)
            s = act.did(nc.scalar.activation(ln_sd[:, :], ln_var[:, :], ACT.Sqrt))
            dve.after(s)
            s = dve.did(nc.vector.reciprocal(ln_r0[:, :], ln_sd[:, :]))
            dve.after(s)
            s = dve.did(nc.vector.tensor_tensor(ln_t[:, :], ln_r0[:, :], ln_r0[:, :], ALU.mult))
            dve.after(s)
            s = dve.did(nc.vector.scalar_tensor_tensor(ln_t[:, :], ln_t[:, :], -0.5, ln_var[:, :], ALU.mult, ALU.mult))
            dve.after(s)
            s = dve.did(nc.vector.scalar_tensor_tensor(ln_rs[:, :], ln_t[:, :], 1.5, ln_r0[:, :], ALU.add, ALU.mult))
            dve.after(s, free)
            for t in range(NT):
                s = dve.did(nc.vector.tensor_scalar(dst(t), src(t), ln_mv[:, t, 0:1], ln_rs[:, t:t + 1],
                                                    ALU.subtract, ALU.mult))
            return s

        for lane in lanes:
            lane.phase("project")

        x_in = [transfers(f"x_in{b}") for b in range(B)]
        x_dram = d["x"].rearrange("b (t p) n -> b p t n", p=P)
        for b in range(B):
            x_in[b].start(sp, x[:, NT * b:NT * b + NT, :], x_dram[b])
        s = pool.did(nc.gpsimd.memset(ident[:, :], 0.0))
        pool.after(s)
        s = pool.did(nc.gpsimd.affine_select(out=ident[:, :], in_=ident[:, :], compare_op=ALU.not_equal, fill=1.0,
                                             base=0, pattern=[[-1, P]], channel_multiplier=1))
        pool.after(s)
        ident_ready = pool.did(nc.gpsimd.tensor_copy(ident_bf[:, :], ident[:, :]))

        attn_a = ctx.enter_context(ExitStack())
        v_a = sb(attn_a, "v_a", [P, B, NT, HA, 2])
        qs = sb(attn_a, "qs", [STACK, B, 2, S], F32R)
        ks = sb(attn_a, "ks", [STACK, B, 2, S])
        mask = sb(attn_a, "mask", [P, B * NT, S], BF16)
        own_head = sb(attn_a, "own_head", [STACK, 16])
        wout_t = sb(attn_a, "wout_t", [KA + 1, D])
        small_a = transfers("small_a")
        small_a.start(act, own_head[:, :], d["own_head"])
        small_a.start(act, wout_t[0:KA, :], d["wout_t"])
        small_a.start(act, wout_t[KA:KA + 1, :], d["bout"])

        pair = ctx.enter_context(ExitStack())
        h_neg = sb(pair, "h_neg", [F1, B * S])
        h_b1 = sb(pair, "h_b1", [F1, B * S])
        w2_t = sb(pair, "w2_t", [F1, F2])
        b2_twice = sb(pair, "b2_twice", [P, 1])
        w3_slide = sb(pair, "w3_slide", [P, 62])
        b3_all = sb(pair, "b3_all", [P, 1])
        small_pair = transfers("small_pair")
        small_pair.start(act, w2_t[:, :], d["w2_t"])
        for half in range(2):
            small_pair.start(act, b2_twice[F2 * half:F2 * half + F2, :], d["b2"])
        small_pair.start(act, b3_all[:, :], d["b3"].partition_broadcast(P))
        s = pool.did(nc.gpsimd.memset(w3_slide[:, :], 0.0))
        act.after(s)
        for half in range(2):
            small_pair.start(act, w3_slide[F2 * half:F2 * half + F2, 30 + half:31 + half], d["w3_t"])

        with ExitStack() as mem:
            y = sb(mem, "y", [P, 2, NT, D])
            z = sb(mem, "z", [P, 2, NT, D])
            xn_t = sb(mem, "xn_t", [P, 2, ND, S])
            gamma = sb(mem, "gamma", [P, ND])
            beta = sb(mem, "beta", [P, ND])
            w1_t = sb(mem, "w1_t", [P, ND, F1])
            b1 = sb(mem, "b1", [F1, 1])
            wqkv_t = sb(mem, "wqkv_t", [P, ND, 3 * KA])
            b_qk = sb(mem, "b_qk", [P, 1])
            b_v = sb(mem, "b_v", [P, KA])
            qk = sb(mem, "qk", [P, 2, S])
            qk_hi = sb(mem, "qk_hi", [P, 2, S], F32R)
            qk_lo = sb(mem, "qk_lo", [P, 2, S], F32R)
            weights = transfers("weights_a")
            for out, name in ((gamma, "gamma"), (beta, "beta"), (w1_t, "w1_t"), (b1, "b1"), (wqkv_t, "wqkv_t"),
                              (b_qk, "b_qk")):
                weights.start(act, out[:], d[name])
            weights.start(act, b_v[:, :], d["b_v"].partition_broadcast(P))
            s_stack = transfers("stacks")
            pool.after(pool.last)
            q_zero = pool.did(nc.gpsimd.memset(qs[96:STACK, :, :, :].bitcast(F32), 0.0))
            pool.after(q_zero)
            k_one = pool.did(nc.gpsimd.memset(ks[96:STACK, :, :, :], 1.0))

            bank_read = [None] * 8
            z_read, xn_read, stack_sent, y_read = [None] * 2, [None] * 2, [None] * 2, [None] * 2
            stack_dmas = [transfers("stacks_even"), transfers("stacks_odd")]
            for b in range(B):
                w = b % 2
                y_ready = layer_norm(lambda t: x[:, NT * b + t, :], lambda t: y[:, w, t, :], x_in[b].all(), y_read[w])
                z_ready = layer_norm(lambda t: y[:, w, t, :], lambda t: z[:, w, t, :], y_ready, z_read[w])
                pool.after(z_ready, k_one)
                for t in range(NT):
                    y_read[w] = pool.did(nc.gpsimd.tensor_tensor(x[:, NT * b + t, :], x[:, NT * b + t, :], y[:, w, t, :],
                                                                 ALU.add))
                pe.after(z_ready, ident_ready)
                act.after(weights.all(), xn_read[w])
                for k in range(ND):
                    pe.after(bank_read[k])
                    for t in range(NT):
                        s = nc.tensor.transpose(ps[:, k, t * P:t * P + P], z[:, w, t, k * P:k * P + P], ident[:, :])
                    s = pe.did(s)
                    act.after(s)
                    xn_ready = bank_read[k] = act.did(nc.scalar.activation(
                        xn_t[:, w, k, :], ps[:, k, :], ACT.Identity, bias=beta[:, k:k + 1], scale=gamma[:, k:k + 1]))
                z_read[w] = s
                pe.after(xn_ready, weights.all(), bank_read[4])
                for k in range(ND):
                    s = nc.tensor.matmul(ps[:, 4, :], w1_t[:, ND - 1 - k, :], xn_t[:, w, ND - 1 - k, :], start=k == 0, stop=k == ND - 1)
                h_done = pe.did(s)
                pe.after(bank_read[5])
                for k in range(ND):
                    s = nc.tensor.matmul(ps[:, 5, :], wqkv_t[:, k, 0:2 * KA], xn_t[:, w, k, :], start=k == 0,
                                         stop=k == ND - 1)
                qk_done = pe.did(s)
                pe.after(bank_read[6])
                for t in range(NT):
                    for k in range(ND):
                        s = nc.tensor.matmul(ps[:, 6, t * KA:t * KA + KA], xn_t[:, w, k, t * P:t * P + P],
                                             wqkv_t[:, k, 2 * KA:3 * KA], start=k == 0, stop=k == ND - 1)
                v_done = xn_read[w] = pe.did(s)
                act.after(h_done)
                s = act.did(nc.scalar.activation(h_neg[:, b * S:b * S + S], ps[:, 4, :], ACT.Copy, scale=-1.0))
                dve.after(s, weights.all())
                bank_read[4] = dve.did(nc.vector.tensor_scalar(h_b1[:, b * S:b * S + S], ps[:, 4, :], b1[:, 0:1], None,
                                                               ALU.add))
                act.after(qk_done)
                s = bank_read[5] = act.did(nc.scalar.activation(qk[:, w, :], ps[:, 5, :], ACT.Identity,
                                                                bias=b_qk[:, 0:1]))
                dve.after(s, stack_sent[w])
                s = dve.did(nc.vector.tensor_copy(qk_hi[:, w, :], qk[:, w, :]))
                dve.after(s)
                qk_split = dve.did(nc.vector.tensor_tensor(qk_lo[:, w, :], qk[:, w, :], qk_hi[:, w, :].bitcast(F32),
                                                           ALU.subtract))
                dve.after(v_done)
                for t in range(NT):
                    bank_read[6] = dve.did(nc.vector.tensor_tensor(
                        v_a[:, b, t, :, :].rearrange("p h e -> p (h e)"), ps[:, 6, t * KA:t * KA + KA], b_v[:, :],
                        ALU.add))
                sp.after(qk_split)
                for u in range(2):
                    for t, (q_src, k_src) in enumerate(((qk_hi, qk_hi), (qk_lo, qk_hi), (qk_hi, qk_lo))):
                        for e in range(2):
                            for dst, src, first in ((qs, q_src, 0), (ks, k_src, KA)):
                                row = 16 * (2 * t + e)
                                at = first + 32 * u + e
                                stack_sent[w] = stack_dmas[w].start(sp, dst[row:row + 16, b, u, :].bitcast(F32),
                                                                    src[at:at + 31:2, w, :].bitcast(F32))
            stacks_ready = stack_sent
            sp.after(*stack_sent)
            for lane in lanes:
                lane.after(*stack_sent)

        phase("pair")
        with ExitStack() as mem:
            N_PAIR = 16
            pair_in = sb(mem, "pair_in", [F1, N_PAIR, S])
            NG = 4
            pair_mid = sb(mem, "pair_mid", [P, NG, 2, S])
            sim = sb(mem, "sim", [P, 2, S + PAD])
            best = sb(mem, "best", [P, 8])
            in_read = [None] * N_PAIR
            mid_read = [None] * NG
            group_read = [None] * 3
            sim_bank_read = [None] * 2
            sim_free = [None] * 2
            for lane in (pe, act, dve):
                lane.after(small_pair.all())

            def row_of(tile, r, c, half):
                return tile * P + 32 * c + 2 * r + half

            def top_k(tile, sim_ready):
                w = tile % 2
                row = sim[:, w, :]

                def round_(n):
                    def go():
                        dve.after(sim_ready if n == 0 else dve.last)
                        s = dve.did(nc.vector.max(best[:, :], row))
                        dve.after(s)
                        dve.did(nc.vector.match_replace(row, best[:, :], row, TAKEN))
                    return go

                def keep():
                    dve.after(dve.last)
                    sim_free[w] = dve.did(nc.vector.tensor_scalar(mask[:, tile, :], sim[:, w, 0:S], NEVAL, MASKED,
                                                                  ALU.is_gt, ALU.mult))
                return [round_(n) for n in range((TOPK + PAD) // 8)] + [keep]

            rounds = []

            def finish_tile(tile, sims_done):
                w = tile % 2
                act.after(sims_done, sim_free[w])
                s = sim_bank_read[w] = act.did(nc.scalar.activation(sim[:, w, 0:S], ps[:, 6 + w, :], ACT.Identity,
                                                                    bias=b3_all[:, 0:1]))
                pool.after(sim_free[w])
                pool.did(nc.gpsimd.memset(sim[:, w, S:S + PAD], SENTINEL))
                pool.after(s)
                s = pool.did(nc.gpsimd.affine_select(out=sim[:, w, 0:S], in_=sim[:, w, 0:S],
                                                     compare_op=ALU.not_equal, fill=0.0, base=(tile % NT) * P,
                                                     pattern=[[-1, S]], channel_multiplier=1))
                return top_k(tile, s)

            def second_layer(step):
                tile, r, groups = step
                w = tile % 2
                if r == 0:
                    pe.after(sim_bank_read[w])
                for g, (slot, ready) in enumerate(groups):
                    pe.after(ready)
                    for k in range(2):
                        c = 2 * g + k
                        s = nc.tensor.matmul(ps[32 * c:32 * c + 32, 6 + w, :], w3_slide[:, 30 - 2 * r:62 - 2 * r],
                                             pair_mid[:, slot, k, :], start=r == 0, stop=r == 15)
                    mid_read[slot] = s = pe.did(s)
                return s

            behind = None
            n_in = n_group = 0
            for tile in range(B * NT):
                b = tile // NT
                for r in range(16):
                    groups = []
                    for g in range(2):
                        slots = []
                        for k in range(2):
                            for half in range(2):
                                i = row_of(tile, r, 2 * g + k, half)
                                slot = n_in % N_PAIR
                                n_in += 1
                                dve.after(in_read[slot])
                                first_ready = dve.did(nc.vector.tensor_scalar(
                                    pair_in[:, slot, :], h_neg[:, b * S:b * S + S], h_b1[:, i:i + 1], 0.0,
                                    ALU.add, ALU.max))
                                slots.append((slot, k, half))
                        bank = 2 * (n_group % 3)
                        pe.after(group_read[n_group % 3], first_ready)
                        for slot, k, half in slots:
                            s = nc.tensor.matmul(ps[F2 * half:F2 * half + F2, bank + k, :], w2_t[:, :],
                                                 pair_in[:, slot, :], start=True, stop=True)
                        s = pe.did(s)
                        for slot, _, _ in slots:
                            in_read[slot] = s
                        mid = n_group % NG
                        act.after(s, mid_read[mid])
                        ready = group_read[n_group % 3] = act.did(nc.scalar.activation(
                            pair_mid[:, mid, :, :], ps[:, bank:bank + 2, :], ACT.Relu, bias=b2_twice[:, 0:1]))
                        groups.append((mid, ready))
                        n_group += 1
                    if behind:
                        s = second_layer(behind)
                        if behind[1] == 15:
                            rounds += finish_tile(behind[0], s)
                    behind = (tile, r, groups)
                    if r % 2 and rounds:
                        rounds.pop(0)()
            s = second_layer(behind)
            rounds += finish_tile(behind[0], s)
            for go in rounds:
                go()

        pair.close()

        k = Core()
        k.nc, k.d, k.ps, k.x, k.ident, k.ident_bf = nc, d, ps, x, ident, ident_bf
        k.pe, k.dve, k.act, k.pool, k.sp = lanes
        k.sb, k.phase, k.transfers, k.layer_norm = sb, phase, transfers, layer_norm
        k.v_a, k.qs, k.ks, k.mask, k.own_head, k.wout_t, k.small_a = v_a, qs, ks, mask, own_head, wout_t, small_a
        if upto >= 2:
            attention_a(k)
        attn_a.close()
        if upto >= 3:
            feed_forward(k, "ffn1")
        if upto >= 4:
            attention_b(k)
        if upto >= 5:
            feed_forward(k, "ffn2")

        phase("out")
        out_dram = d["out"].rearrange("b (t p) n -> b p t n", p=P)
        stored = transfers("stored")
        for b in range(B):
            stored.start(sp, out_dram[b], x[:, NT * b:NT * b + NT, :])
        if upto == 1:
            stored.start(sp, d["dbg"][0:P, 0:B * NT * S // 2], mask[:, :, :].rearrange("p a b -> p (a b)").bitcast(F32))
        sp.after(stored.all(), small_a.all())


def attention_a(k):
    nc, pe, dve, act, pool, sp, ps, x = k.nc, k.pe, k.dve, k.act, k.pool, k.sp, k.ps, k.x
    k.phase("attn_a")
    LEAD, CHUNK, N_KM, N_EX = 18, 16, 3, (6, 8)
    HEADS = B * HA
    with ExitStack() as mem:
        mask_t = k.sb(mem, "mask_t", [P, 2, NT, S], BF16)
        v_aug = k.sb(mem, "v_aug", [P, 2, NT, HA, 3])
        km = k.sb(mem, "km", [STACK, 2 * N_KM, S], F32R)
        ex = k.sb(mem, "ex", [P, sum(N_EX), 2, S])
        maxes = k.sb(mem, "maxes", [P, 2, NT, CHUNK])
        unused = k.sb(mem, "unused", [P, 2, S], BF16)
        max_t = k.sb(mem, "max_t", [CHUNK, 2, S], F32R)
        ao_t = k.sb(mem, "ao_t", [P, 2, HA // 4, S])
        ao = k.sb(mem, "ao", [P, 2, HA, 2])
        r_den = k.sb(mem, "r_den", [P, HA])
        ao_feat = k.sb(mem, "ao_feat", [KA + 1, 2, P])

        OUT_BANK, SIDE_BANK = 6, 7
        pool.after(k.small_a.all())
        s = pool.did(nc.gpsimd.memset(v_aug[:, :, :, :, 2:3], 1.0))
        pool.after(s)
        one_row = pool.did(nc.gpsimd.memset(ao_feat[KA:KA + 1, :, :], 1.0))
        pool.after(one_row)
        bank_zero = dve.did(nc.vector.memset(ps[:, OUT_BANK, :], 0.0))
        pe.after(k.small_a.all(), bank_zero, one_row)
        for lane in (dve, act):
            lane.after(k.small_a.all())

        n_km = [0, 0]
        km_read = [None] * (2 * N_KM)
        o1_read, o2_read = [None] * 2, [None] * 2
        max_read, max_sent = [None] * 2, [None] * 2
        max_dmas = [k.transfers("maxima_even"), k.transfers("maxima_odd")]
        maxes_ready = {}
        in_place = {}
        mask_ready = [None] * B
        mask_read = [None] * B
        v_ready, v_read = [None] * B, [None] * B
        ex_read = [None] * sum(N_EX)
        ao_read = [None] * 2
        side_read = [None]
        counts = {"o1": 0, "group": 0}

        def one_head(engine, kind, n):
            b, u, a = n // HA, n // CHUNK % 2, n % CHUNK
            slot = kind * N_KM + n_km[kind] % N_KM
            n_km[kind] += 1
            engine.after(km_read[slot])
            own = k.own_head[:, a:a + 1]
            if engine is act:
                return slot, act.did(nc.scalar.activation(km[:, slot, :], k.ks[:, b, u, :], ACT.Copy, scale=own))
            return slot, dve.did(nc.vector.tensor_scalar(km[:, slot, :], k.ks[:, b, u, :], own, None, ALU.mult))

        def stack_of(engine, kind, n):
            made = ahead[kind].pop(n, None) or one_head(engine, kind, n)
            if n + 1 < HEADS:
                ahead[kind][n + 1] = one_head(engine, kind, n + 1)
            return made

        ahead = ({}, {})

        def maxima(n):
            b, u, a, w = n // HA, n // CHUNK % 2, n % CHUNK, n // CHUNK % 2
            slot, ready = stack_of(dve, 0, n)
            if a == 0:
                dve.after(max_read[w])
            for t in range(NT):
                bank = counts["o1"] % 2
                counts["o1"] += 1
                pe.after(ready, o1_read[bank])
                s = pe.did(nc.tensor.matmul(ps[:, bank, :], k.qs[:, b, u, t * P:t * P + P], km[:, slot, :],
                                            start=True, stop=True))
                dve.after(s, o1_read[bank])
                o1_read[bank] = dve.did(nc.vector.tensor_tensor_reduce(
                    unused[:, bank, :], ps[:, bank, :], k.mask[:, NT * b + t, :], 1.0, TAKEN, ALU.add, ALU.max,
                    maxes[:, w, t, a:a + 1]))
                km_read[slot] = s
                maxes_ready[n // CHUNK] = o1_read[bank]
                yield

        def place_maxima(chunk):
            b, u, w = chunk // 2, chunk % 2, chunk % 2
            pe.after(maxes_ready[chunk], side_read[0])
            for t in range(NT):
                s = nc.tensor.transpose(ps[0:CHUNK, SIDE_BANK, t * P:t * P + P], maxes[:, w, t, :], k.ident[:, :])
            s = max_read[w] = pe.did(s)
            act.after(s, max_sent[w])
            s = side_read[0] = act.did(nc.scalar.activation(max_t[:, w, :], ps[0:CHUNK, SIDE_BANK, :], ACT.Copy,
                                                            scale=-1.0))
            sp.after(s, km_read[(n_km[0] - 1) % N_KM])
            in_place[chunk] = max_sent[w] = max_dmas[w].start(sp, k.qs[96:STACK, b, u, :].bitcast(F32),
                                                              max_t[:, w, :].bitcast(F32))

        def turn_mask(b, t):
            w = b % 2
            bank = ps[:, SIDE_BANK, 0:S // 2].bitcast(BF16)
            pe.after(side_read[0])
            for i in range(NT):
                s = nc.tensor.transpose(bank[:, i * P:i * P + P], k.mask[:, NT * b + i, t * P:t * P + P],
                                        k.ident_bf[:, :])
            s = pe.did(s)
            act.after(s, mask_read[b - 2] if b >= 2 else None)
            mask_ready[b] = side_read[0] = act.did(nc.scalar.activation(mask_t[:, w, t, :], bank, ACT.Copy))

        def values(b):
            w = b % 2
            pool.after(v_read[b - 2] if b >= 2 else None)
            v_ready[b] = pool.did(nc.gpsimd.tensor_copy(
                v_aug[:, w, :, :, 0:2].rearrange("p t h e -> p (t h) e"),
                k.v_a[:, b, :, :, :].rearrange("p t h e -> p (t h) e")))

        def exponentials(n, out):
            b, u, w = n // HA, n // CHUNK % 2, (n // HA) % 2
            slot, ready = stack_of(act, 1, n)
            pe.after(ready, in_place[n // CHUNK], mask_ready[b])
            for g in range(NT // 2):
                pair_of_banks, e = counts["group"] % 2, g * N_EX[0] + n % N_EX[g]
                counts["group"] += 1
                bank = 2 + 2 * pair_of_banks
                pe.after(o2_read[pair_of_banks])
                for j in range(2):
                    t = 2 * g + j
                    nc.tensor.matmul(ps[:, bank + j, :], k.ident_bf[:, :], mask_t[:, w, t, :], start=True, stop=False)
                    s = nc.tensor.matmul(ps[:, bank + j, :], km[:, slot, t * P:t * P + P], k.qs[:, b, u, :],
                                         start=False, stop=True)
                s = pe.did(s)
                act.after(s, ex_read[e])
                s2 = o2_read[pair_of_banks] = act.did(nc.scalar.activation(ex[:, e, :, :], ps[:, bank:bank + 2, :], ACT.Exp,
                                                                           scale=2.0 ** -0.5))
                out.append((e, s2))
                km_read[slot] = s
                mask_read[b] = s
                yield

        def weighted(n, groups):
            b, w, block = n // HA, (n // HA) % 2, n % HA // 4
            pe.after(v_ready[b], out_read[0])
            for t in range(NT):
                for g in range(4):
                    e, ready = groups[g][t // 2]
                    pe.after(ready)
                    s = nc.tensor.matmul(ps[32 * g:32 * g + 3, OUT_BANK, :], v_aug[:, w, t, 4 * block + g, :],
                                         ex[:, e, t % 2, :], start=t == 0, stop=t == NT - 1)
                s = pe.did(s)
                for g in groups:
                    ex_read[g[t // 2][0]] = s
                if t < NT - 1:
                    yield
            v_read[b] = s
            act.after(s, ao_read[w] if block == 0 else None)
            s = out_read[0] = act.did(nc.scalar.activation(ao_t[:, w, block, :], ps[:, OUT_BANK, :], ACT.Copy))
            if block == HA // 4 - 1:
                side[:0] = finish(b, s)
            yield

        out_read = [bank_zero]

        def finish(b, ao_ready):
            w = b % 2
            steps = []
            for t in range(NT):
                for half in range(2):
                    def divide(t=t, half=half):
                        pe.after(ao_ready, side_read[0])
                        for i in range(4):
                            s = nc.tensor.transpose(ps[:, SIDE_BANK, i * P:i * P + P],
                                                    ao_t[:, w, 4 * half + i, t * P:t * P + P], k.ident[:, :])
                        s = pe.did(s)
                        ao_read[w] = s
                        sums = ps[:, SIDE_BANK, :].rearrange("p (h r) -> p h r", r=32)
                        part = r_den[:, 16 * half:16 * half + 16]
                        dve.after(s)
                        s = dve.did(nc.vector.reciprocal(part, sums[:, :, 2]))
                        dve.after(s)
                        for e in range(2):
                            s = dve.did(nc.vector.tensor_tensor(ao[:, t % 2, 16 * half:16 * half + 16, e], sums[:, :, e],
                                                                part, ALU.mult))
                        side_read[0] = k.ao_done = s
                    steps.append(divide)

                def turn(t=t):
                    pe.after(k.ao_done, side_read[0])
                    s = pe.did(nc.tensor.transpose(ps[0:KA, SIDE_BANK, 0:P],
                                                   ao[:, t % 2, :, :].rearrange("p h e -> p (h e)"), k.ident[:, :]))
                    act.after(s)
                    side_read[0] = k.feat_done = act.did(nc.scalar.activation(ao_feat[0:KA, t % 2, :],
                                                                              ps[0:KA, SIDE_BANK, 0:P], ACT.Copy))
                steps.append(turn)

                def project(t=t):
                    pe.after(k.feat_done, side_read[0])
                    s = pe.did(nc.tensor.matmul(ps[:, SIDE_BANK, :], ao_feat[:, t % 2, :], k.wout_t[:, :], start=True,
                                                stop=True))
                    dve.after(s)
                    side_read[0] = dve.did(nc.vector.tensor_tensor(x[:, NT * b + t, :], x[:, NT * b + t, :],
                                                                   ps[:, SIDE_BANK, :], ALU.add))
                steps.append(project)
            return steps

        side = []
        values(0)
        for t in range(NT):
            turn_mask(0, t)
        for n in range(LEAD):
            for _ in maxima(n):
                pass
            if n == CHUNK:
                place_maxima(0)
        groups = []
        behind = iter(())
        for n in range(HEADS + 4):
            b, h = n // HA, n % HA
            if h == 4 and b + 1 < B:
                values(b + 1)
                side += [lambda t=t, b=b: turn_mask(b + 1, t) for t in range(NT)]
            groups.append([])
            ahead_steps = maxima(n + LEAD) if n + LEAD < HEADS else iter(())
            own_steps = exponentials(n, groups[-1]) if n < HEADS else iter(())
            for steps in (own_steps, ahead_steps, behind, ahead_steps, own_steps, ahead_steps):
                next(steps, None)
            if side:
                side.pop(0)()
            for _ in ahead_steps:
                pass
            next(own_steps, None)
            if (n + LEAD) % CHUNK == 0 and n + LEAD <= HEADS:
                place_maxima((n + LEAD) // CHUNK - 1)
            if h % 4 == 3:
                behind, groups = weighted(n - 3, groups), []
        for step in side:
            step()


def feed_forward(k, name):
    nc, pe, dve, act, pool, sp, ps, x = k.nc, k.pe, k.dve, k.act, k.pool, k.sp, k.ps, k.x
    k.phase(name)
    OC = 2
    CHUNKS = NI // OC
    WU, WD = ND * 2 * OC * P, OC * D
    with ExitStack() as mem:
        raw = k.sb(mem, name + "_raw", [P, 2, WU + WD])
        w_hi = k.sb(mem, name + "_w_hi", [P, 2, WU + WD], F32R)
        w_lo = k.sb(mem, name + "_w_lo", [P, 2, WU + WD], F32R)
        z = k.sb(mem, name + "_z", [P, NT, D])
        z_hi = k.sb(mem, name + "_z_hi", [P, ND, B * S], F32R)
        z_lo = k.sb(mem, name + "_z_lo", [P, ND, B * S], F32R)
        silu = k.sb(mem, name + "_silu", [P, 2, S])
        inner = k.sb(mem, name + "_inner", [P, 2, S])
        in_hi = k.sb(mem, name + "_in_hi", [P, 2, OC, S], F32R)
        in_lo = k.sb(mem, name + "_in_lo", [P, 2, OC, S], F32R)
        loads = [k.transfers(f"{name}_w{i}") for i in range(2)]
        w_read = [None] * 2
        raw_read = [[], []]
        w_ready = {}
        z_ready, z_free = {}, None
        bank_read = [None] * 8
        silu_read, in_read = [None] * 2, [None] * 2

        def load(c):
            w = c % 2
            sp.after(*raw_read[w])
            return loads[w].start(sp, raw[:, w, :], k.d["w_ffn"][c])

        def split(c, arrived):
            w = c % 2
            act.after(arrived, w_read[w])
            for a, e in ((0, WU // 2), (WU // 2, WU), (WU, WU + WD)):
                s = act.did(nc.scalar.activation(w_hi[:, w, a:e], raw[:, w, a:e], ACT.Copy))
                pool.after(s)
                s = pool.did(nc.gpsimd.tensor_tensor(w_lo[:, w, a:e], raw[:, w, a:e], w_hi[:, w, a:e].bitcast(F32),
                                                     ALU.subtract))
            raw_read[w] = [s]
            w_ready[c] = s

        def normed(b):
            s = k.layer_norm(lambda t: x[:, NT * b + t, :], lambda t: z[:, t, :], x_done[b], z_read[0])
            pe.after(s)
            for f in range(ND):
                bank = 6 + f % 2
                pe.after(bank_read[bank])
                for t in range(NT):
                    s = nc.tensor.transpose(ps[:, bank, t * P:t * P + P], z[:, t, f * P:f * P + P], k.ident[:, :])
                s = z_read[0] = pe.did(s)
                act.after(s)
                at = slice(b * S, b * S + S)
                s = act.did(nc.scalar.activation(z_hi[:, f, at], ps[:, bank, :], ACT.Copy))
                dve.after(s)
                bank_read[bank] = z_ready[b] = dve.did(nc.vector.tensor_tensor(
                    z_lo[:, f, at], ps[:, bank, :], z_hi[:, f, at].bitcast(F32), ALU.subtract))

        def up(c, b, o):
            w = c % 2
            for g in range(2):
                bank = 2 * (o % 2) + g
                pe.after(bank_read[bank])
                n = 0
                for z_part, w_part in ((z_hi, w_hi), (z_lo, w_hi), (z_hi, w_lo)):
                    for f in range(ND):
                        at = (f * 2 + g) * OC * P + o * P
                        s = nc.tensor.matmul(ps[:, bank, :], w_part[:, w, at:at + P], z_part[:, f, b * S:b * S + S],
                                             start=n == 0, stop=n == 3 * ND - 1)
                        n += 1
                s = pe.did(s)
                if g == 0:
                    act.after(s, silu_read[o % 2])
                    gate = bank_read[bank] = act.did(nc.scalar.activation(silu[:, o % 2, :], ps[:, bank, :], ACT.Silu))
            u = (c * B + b) % 2
            dve.after(s, gate)
            s = silu_read[o % 2] = bank_read[bank] = dve.did(nc.vector.tensor_tensor(
                inner[:, o % 2, :], silu[:, o % 2, :], ps[:, bank, :], ALU.mult))
            dve.after(s, in_read[u])
            s = dve.did(nc.vector.tensor_copy(in_hi[:, u, o, :], inner[:, o % 2, :]))
            dve.after(s)
            return dve.did(nc.vector.tensor_tensor(in_lo[:, u, o, :], inner[:, o % 2, :], in_hi[:, u, o, :].bitcast(F32),
                                                   ALU.subtract))

        def down(c, b, t, ready):
            w, u = c % 2, (c * B + b) % 2
            bank = 4 + t % 2
            pe.after(ready, bank_read[bank])
            n = 0
            for i_part, w_part in ((in_hi, w_hi), (in_lo, w_hi), (in_hi, w_lo)):
                for o in range(OC):
                    s = nc.tensor.matmul(ps[:, bank, :], i_part[:, u, o, t * P:t * P + P],
                                         w_part[:, w, WU + o * D:WU + o * D + D], start=n == 0, stop=n == 3 * OC - 1)
                    n += 1
            s = pe.did(s)
            in_read[u] = s
            if b == B - 1:
                w_read[w] = s
            dve.after(s, x_done[b])
            bank_read[bank] = dve.did(nc.vector.tensor_tensor(x[:, NT * b + t, :], x[:, NT * b + t, :], ps[:, bank, :],
                                                              ALU.add))
            return bank_read[bank]

        z_read = [None]
        x_done = [None] * B
        arrived = [load(0), load(1)]
        split(0, arrived[0])
        normed(0)
        behind = None
        for c in range(CHUNKS):
            for b in range(B):
                pe.after(w_ready[c], z_ready[b])
                for o in range(OC):
                    s = up(c, b, o)
                    if behind:
                        for t in range(2 * o, 2 * o + 2):
                            s_x = down(*behind[:2], t, behind[2])
                        if o == OC - 1:
                            x_done[behind[1]] = s_x
                behind = (c, b, s)
                if c == 0 and b + 1 < B:
                    normed(b + 1)
                if b == 0 and c + 1 < CHUNKS:
                    split(c + 1, arrived[(c + 1) % 2])
                    if c + 2 < CHUNKS:
                        arrived[c % 2] = load(c + 2)
        for t in range(NT):
            down(*behind[:2], t, behind[2])


def attention_b(k):
    nc, pe, dve, act, pool, sp, ps, x, d = k.nc, k.pe, k.dve, k.act, k.pool, k.sp, k.ps, k.x, k.d
    k.phase("attn_b")
    ROWS, N_EX, HU, SCALE = 97, 12, 4, HDB ** -0.5
    UNITS = B * (HB // HU)
    with ExitStack() as mem:
        w_qk = k.sb(mem, "wb_qk", [P, ND, HB // HU, 2, P])
        w_v = k.sb(mem, "wb_v", [P, ND, D])
        w_proj = k.sb(mem, "wb_proj", [P, ND, D])
        z = k.sb(mem, "zb", [P, NT, D])
        z_t = k.sb(mem, "zb_t", [P, ND, S])
        qk = k.sb(mem, "qk_b", [P, 2, S])
        hi = k.sb(mem, "hi_b", [P, 2, S], F32R)
        lo = k.sb(mem, "lo_b", [P, 2, S], F32R)
        q_stack = k.sb(mem, "q_stack", [ROWS, 3, HU, S], F32R)
        k_stack = k.sb(mem, "k_stack", [ROWS, 3, HU, S], F32R)
        v = k.sb(mem, "vb", [P, 2, NT, D])
        ex = k.sb(mem, "ex_b", [P, N_EX, S])
        out_t = k.sb(mem, "out_t", [P, ND, S])
        r_den = k.sb(mem, "r_den_b", [P, S])
        maxes = k.sb(mem, "maxes_b", [P, 2, HU, NT])
        max_t = k.sb(mem, "max_t_b", [HU, 2, S], F32R)
        ones = k.sb(mem, "ones_b", [P, 32])
        lam_in = z[0:1, :, :]
        lam_unused = z_t[0:1, :, :]
        lam = k.sb(mem, "lam", [1, 4])
        q2_row = k.sb(mem, "q2_row", [1, P])
        q1_col = k.sb(mem, "q1_col", [P, 1])
        q_scale = k.sb(mem, "q_scale", [P, 1])

        O2_BANKS, SUM_BANK, DEN_BANK, SIDE_BANK = (2, 3, 4), 5, 6, 7
        small = k.transfers("small_b")
        small.start(act, lam_in[:, :, :], d["lambdas"])
        small.start(act, q2_row[:, :], d["q2_row"])
        small.start(act, q1_col[:, :], d["q1_col"])
        weights = k.transfers("weights_b")
        weights.start(sp, w_qk[:, :, :, :, :], d["wb_qk"])
        weights.start(sp, w_v[:, :, :], d["wb_v"])
        weights.start(sp, w_proj[:, :, :], d["wb_proj"])

        dve.after(small.all())
        for i in range(2):
            s = dve.did(nc.vector.tensor_tensor_reduce(lam_unused[:, i, :], lam_in[:, 2 * i, :], lam_in[:, 2 * i + 1, :],
                                                       1.0, 0.0, ALU.mult, ALU.add, lam[:, i:i + 1]))
        act.after(s)
        s = act.did(nc.scalar.activation(lam[:, 2:4], lam[:, 0:2], ACT.Exp))
        dve.after(s)
        s = dve.did(nc.vector.tensor_tensor(lam[:, 0:1], lam[:, 3:4], lam[:, 2:3], ALU.subtract))
        dve.after(s)
        s = dve.did(nc.vector.tensor_scalar(lam[:, 1:2], lam[:, 0:1], -LAMBDA_INIT, None, ALU.add))
        pe.after(s)
        s = pe.did(nc.tensor.matmul(ps[:, SIDE_BANK, 0:1], q2_row[:, :], lam[:, 1:2], start=True, stop=True))
        dve.after(s)
        q_scale_ready = dve.did(nc.vector.tensor_tensor(q_scale[:, :], ps[:, SIDE_BANK, 0:1], q1_col[:, :], ALU.add))
        s = pool.did(nc.gpsimd.memset(ones[:, :], 1.0))
        pool.after(s)
        s = pool.did(nc.gpsimd.memset(k_stack[96:97, :, :, :].bitcast(F32), 1.0))
        ones_ready = s

        side_read = [q_scale_ready]
        z_read, z_t_read, qk_read, z_t_ready = [None], [None], [None], [None]
        o1_read, o2_read = [None] * 2, [None] * 3
        ex_read = [None] * N_EX
        v_ready, v_read = [None] * B, [None] * B
        sum_read, den_read, out_read = [ones_ready], [None], [None]
        split_done = [None] * UNITS
        stack_dmas = [k.transfers(f"stacks_b{i}") for i in range(3)]
        max_dmas = [k.transfers("maxima_b_even"), k.transfers("maxima_b_odd")]
        stacked, hi_sent = [None] * UNITS, [None]
        in_place = [None] * UNITS
        zeroed = [None] * 3
        o1_last, o2_last = [None] * UNITS, [None] * UNITS
        max_read = [None] * 2
        n_o2 = [0]
        project_last = [None] * B

        def norm_steps(b):
            def norm():
                z_read.append(k.layer_norm(lambda t: x[:, NT * b + t, :], lambda t: z[:, t, :], None, z_read[0]))
            steps = [norm]
            for f in range(ND):
                def turn(f=f):
                    pe.after(z_read[-1], side_read[0])
                    for t in range(NT):
                        s = nc.tensor.transpose(ps[:, SIDE_BANK, t * P:t * P + P], z[:, t, f * P:f * P + P], k.ident[:, :])
                    s = z_read[0] = pe.did(s)
                    act.after(s, z_t_read[0])
                    side_read[0] = z_t_ready[0] = act.did(nc.scalar.activation(z_t[:, f, :], ps[:, SIDE_BANK, :], ACT.Copy))
                steps.append(turn)
            for t in range(NT):
                def values(t=t):
                    pe.after(z_t_ready[0], side_read[0], weights.all())
                    for f in range(ND):
                        s = nc.tensor.matmul(ps[:, SIDE_BANK, :], z_t[:, f, t * P:t * P + P], w_v[:, f, :],
                                             start=f == 0, stop=f == ND - 1)
                    s = pe.did(s)
                    act.after(s, v_read[b - 2] if b >= 2 else None)
                    side_read[0] = v_ready[b] = act.did(nc.scalar.activation(v[:, b % 2, t, :], ps[:, SIDE_BANK, :],
                                                                             ACT.Copy))
                steps.append(values)
            return steps

        def query_key_steps(n):
            c, w = n % (HB // HU), n % 3
            steps = []
            for i in range(2):
                def product(i=i):
                    pe.after(z_t_ready[0], side_read[0], weights.all())
                    for f in range(ND):
                        s = nc.tensor.matmul(ps[:, SIDE_BANK, :], w_qk[:, f, c, i, :], z_t[:, f, :], start=f == 0,
                                             stop=f == ND - 1)
                    s = pe.did(s)
                    z_t_read[0] = s
                    act.after(s, qk_read[0], q_scale_ready)
                    side_read[0] = split_done[n] = act.did(nc.scalar.activation(
                        qk[:, i, :], ps[:, SIDE_BANK, :], ACT.Copy, scale=1.0 if i else q_scale[:, 0:1]))
                steps.append(product)

            def split():
                dve.after(split_done[n], hi_sent[0])
                s = dve.did(nc.vector.tensor_copy(hi[:, :, :], qk[:, :, :]))
                dve.after(s)
                s = qk_read[0] = dve.did(nc.vector.tensor_tensor(lo[:, :, :], qk[:, :, :], hi[:, :, :].bitcast(F32),
                                                                 ALU.subtract))
                sp.after(s, o2_last[n - 3] if n >= 3 else None, ones_ready)
                for g in range(HU):
                    for r, (q_part, k_part) in enumerate(((hi, hi), (lo, hi), (hi, lo))):
                        for stack, part, i in ((q_stack, q_part, 0), (k_stack, k_part, 1)):
                            stacked[n] = stack_dmas[w].start(sp, stack[32 * r:32 * r + 32, w, g, :].bitcast(F32),
                                                             part[32 * g:32 * g + 32, i, :].bitcast(F32))
                hi_sent[0] = stacked[n]
                pool.after(o2_last[n - 3] if n >= 3 else None, ones_ready)
                zeroed[w] = pool.did(nc.gpsimd.memset(q_stack[96:97, w, :, :].bitcast(F32), 0.0))
            return steps + [split]

        def maxima(n):
            w, s3 = n % 2, n % 3
            pe.after(stacked[n], zeroed[s3])
            dve.after(max_read[w])
            for i in range(HU * NT):
                g, t = i // NT, i % NT
                pe.after(o1_read[i % 2])
                s = pe.did(nc.tensor.matmul(ps[:, i % 2, :], q_stack[:, s3, g, t * P:t * P + P], k_stack[:, s3, g, :],
                                            start=True, stop=True))
                dve.after(s)
                o1_read[i % 2] = dve.did(nc.vector.tensor_reduce(maxes[:, w, g, t:t + 1], ps[:, i % 2, :], AX.X, ALU.max))
                o1_last[n] = s
                yield

        def place_maxima(n):
            w = n % 2
            pe.after(*o1_read, side_read[0])
            for t in range(NT):
                s = nc.tensor.transpose(ps[0:HU, SIDE_BANK, t * P:t * P + P], maxes[:, w, :, t], k.ident[:, :])
            s = max_read[w] = pe.did(s)
            act.after(s, in_place[n - 2] if n >= 2 else None)
            s = side_read[0] = act.did(nc.scalar.activation(max_t[:, w, :], ps[0:HU, SIDE_BANK, :], ACT.Copy,
                                                            scale=-1.0))
            sp.after(s, o1_last[n])
            for g in range(HU):
                in_place[n] = max_dmas[w].start(sp, q_stack[96:97, n % 3, g, :].bitcast(F32),
                                                max_t[g:g + 1, w, :].bitcast(F32))

        def exponentials(n, tiles):
            w = n % 3
            pe.after(in_place[n])
            for t in range(NT):
                for g in range(HU):
                    o, e = n_o2[0] % 3, n_o2[0] % N_EX
                    n_o2[0] += 1
                    bank = O2_BANKS[o]
                    pe.after(o2_read[o])
                    s = o2_last[n] = pe.did(nc.tensor.matmul(ps[:, bank, :], k_stack[:, w, g, t * P:t * P + P],
                                                             q_stack[:, w, g, :], start=True, stop=True))
                    act.after(s, ex_read[e])
                    s = o2_read[o] = act.did(nc.scalar.activation(ex[:, e, :], ps[:, bank, :], ACT.Exp, scale=SCALE))
                    tiles.append((e, s))
                    yield

        def weighted(n, tiles):
            b, c = n // (HB // HU), n % (HB // HU)
            pe.after(v_ready[b], sum_read[0], den_read[0])
            for t in range(NT):
                for bank, of_values in ((SUM_BANK, True), (DEN_BANK, False)):
                    for g in range(HU):
                        e, ready = tiles[HU * t + g]
                        pe.after(ready)
                        at = P * c + 32 * g
                        s = nc.tensor.matmul(ps[32 * g:32 * g + 32, bank, :],
                                             v[:, b % 2, t, at:at + 32] if of_values else ones[:, :], ex[:, e, :],
                                             start=t == 0, stop=t == NT - 1)
                    s = pe.did(s)
                    if not of_values:
                        for g in range(HU):
                            ex_read[tiles[HU * t + g][0]] = s
                    if of_values or t < NT - 1:
                        yield
            v_read[b] = s
            dve.after(s, sum_read[0], out_read[0])
            s = den_read[0] = dve.did(nc.vector.reciprocal(r_den[:, :], ps[:, DEN_BANK, :]))
            dve.after(s)
            s = sum_read[0] = dve.did(nc.vector.tensor_tensor(out_t[:, c, :], ps[:, SUM_BANK, :], r_den[:, :],
                                                              ALU.mult))
            if c == HB // HU - 1:
                side.extend(project_steps(b, s))
            yield

        def project_steps(b, ready):
            steps = []
            for t in range(NT):
                def go(t=t):
                    pe.after(ready, side_read[0])
                    for c in range(ND):
                        s = nc.tensor.matmul(ps[:, SIDE_BANK, :], out_t[:, c, t * P:t * P + P], w_proj[:, c, :],
                                             start=c == 0, stop=c == ND - 1)
                    s = out_read[0] = pe.did(s)
                    dve.after(s)
                    side_read[0] = dve.did(nc.vector.scalar_tensor_tensor(
                        x[:, NT * b + t, :], ps[:, SIDE_BANK, :], 1.0 - LAMBDA_INIT, x[:, NT * b + t, :], ALU.mult,
                        ALU.add))
                steps.append(go)
            return steps

        side = norm_steps(0) + query_key_steps(0)
        for step in side:
            step()
        side = []
        tiles, behind = {}, iter(())
        for n in range(UNITS + 2):
            if n + 1 < UNITS:
                if (n + 1) % (HB // HU) == 0:
                    side += norm_steps((n + 1) // (HB // HU))
                side += query_key_steps(n + 1)
            rows = maxima(n) if n < UNITS else iter(())
            if n == UNITS:
                pass
            tiles[n - 1] = []
            own = exponentials(n - 1, tiles[n - 1]) if 1 <= n <= UNITS else iter(())
            sums = weighted(n - 1, tiles[n - 1]) if 1 <= n <= UNITS else iter(())
            for i in range(HU * NT + 4):
                next(own, None)
                next(rows, None)
                if i >= HU and i % 2 == 0:
                    next(sums, None)
                if side and (i % 2 or len(side) > 8):
                    side.pop(0)()
            for _ in sums:
                pass
            for step in side:
                step()
            side.clear()
            if n < UNITS:
                place_maxima(n)


def layout(inputs):
    import numpy as np

    def of(name):
        return np.asarray(inputs["L0_" + name])

    def feature_major(w):
        return w.T.reshape(ND, P, -1).transpose(1, 0, 2)

    a = {"x": of("attn_a_x")}
    a["gamma"] = of("attn_a_gamma").reshape(ND, P).T
    a["beta"] = of("attn_a_beta").reshape(ND, P).T
    a["w1_t"] = feature_major(of("attn_a_W1"))
    a["b1"] = of("attn_a_b1")[:, None]
    a["w2_t"] = of("attn_a_W2").T
    a["b2"] = of("attn_a_b2")[:, None]
    a["w3_t"] = of("attn_a_W3").T
    a["b3"] = of("attn_a_b3")
    a["wqkv_t"] = feature_major(of("attn_a_Wqkv"))
    a["b_qk"] = of("attn_a_bqkv")[:2 * KA, None]
    a["b_v"] = of("attn_a_bqkv")[2 * KA:]
    a["wout_t"] = of("attn_a_Wout").T
    a["bout"] = of("attn_a_bout")[None]
    a["own_head"] = np.tile(np.eye(16, dtype=np.float32), (STACK // 16, 1))

    oc, chunks = 2, NI // 2
    up = of("ffn_w_gate_up").reshape(2, chunks, oc, P, ND, P).transpose(1, 5, 4, 0, 2, 3).reshape(chunks, P, -1)
    down = of("ffn_w_down").T.reshape(chunks, oc, P, D).transpose(0, 2, 1, 3).reshape(chunks, P, -1)
    a["w_ffn"] = np.concatenate([up, down], axis=-1)

    w = of("attn_b_W_attn").reshape(ND, P, 3 * D).transpose(1, 0, 2)
    q1, k1, q2, k2 = (w[:, :, i * D // 2:(i + 1) * D // 2].reshape(P, ND, HB // 4, 4, HDB) for i in range(4))
    q = np.stack([q1, q2], axis=4).reshape(P, ND, HB // 4, P)
    k = np.stack([k1, k2], axis=4).reshape(P, ND, HB // 4, P)
    a["wb_qk"] = np.stack([q, k], axis=3)
    a["wb_v"] = w[:, :, 2 * D:]
    a["wb_proj"] = of("attn_b_W_proj").reshape(ND, P, D).transpose(1, 0, 2)
    a["lambdas"] = np.stack([of("attn_b_lambda_" + n) for n in ("q1", "k1", "q2", "k2")])[None]
    second = (np.arange(P) // HDB % 2).astype(np.float32)
    a["q2_row"] = second[None]
    a["q1_col"] = (np.arange(P) // HDB % 2 == 0).astype(np.float32)[:, None]
    return {name: np.ascontiguousarray(v) for name, v in a.items()}


def kernel(**inputs):
    import concourse.bacc as bacc
    from concourse.bass_utils import run_bass_kernel_spmd

    arrays = {"in_" + name: v for name, v in layout(inputs).items()}
    nc = bacc.Bacc("TRN2", target_bir_lowering=False, num_devices=1)
    d = {name[3:]: nc.dram_tensor(name, v.shape, mybir.dt.from_np(v.dtype), kind="ExternalInput").ap()
         for name, v in arrays.items()}
    d["out"] = nc.dram_tensor("out", (B, S, D), F32, kind="ExternalOutput").ap()
    build(nc, d)
    return run_bass_kernel_spmd(nc, [arrays], core_ids=[0]).results[0]["out"]
```

```python
from contextlib import ExitStack

import concourse.bass as bass
from concourse import mybir

ALU = mybir.AluOpType
ACT = mybir.ActivationFunctionType
AX = mybir.AxisListType
F32 = mybir.dt.float32
F32R = mybir.dt.float32r
BF16 = mybir.dt.bfloat16

P = 128
B, S, D = 4, 512, 512
NT = S // P
ND = D // P
F1, F2 = 128, 64
TOPK = max(1, int(S * 0.1))
HA, KA = 32, 64
HB, HDB = 16, 16
INTER = 2048
NI = INTER // P
LN_EPS = 1e-5
LAMBDA_INIT = 0.8 - 0.6 * 1.0
MASKED = -1e30
TAKEN = -3e38
SENTINEL = 3e38
NEVAL = -2.9e38
PAD = (-TOPK) % 8
HALVES = 6
STACK = 16 * (HALVES + 1)


class Lane:

    def __init__(self, nc, ctx, engine, name):
        self.nc, self.ctx, self.engine, self.name = nc, ctx, engine, name
        self.waited = {}
        self.last = None

    def phase(self, name):
        self.sem_name = f"{self.name}_{name}"
        self.sem = self.ctx.enter_context(self.nc.semaphore(self.sem_name))
        self.count = 0

    def did(self, instruction):
        self.count += 1
        instruction.then_inc(self.sem, 1)
        self.last = (self.sem_name, self.sem, self.count)
        return self.last

    def after(self, *signals):
        for signal in signals:
            if signal is None:
                continue
            name, sem, value = signal
            if self.waited.get(name, 0) < value:
                self.engine.wait_ge(sem, value)
                self.waited[name] = value


class Transfers:

    def __init__(self, nc, ctx, name):
        self.name, self.sem, self.count = name, ctx.enter_context(nc.semaphore(name)), 0

    def start(self, lane, out, in_):
        self.count += 16
        lane.engine.dma_start(out, in_).then_inc(self.sem, 16)
        return self.all()

    def all(self):
        return (self.name, self.sem, self.count)


class Core:
    pass


def build(nc, d, upto=9):
    with ExitStack() as ctx:
        pe = Lane(nc, ctx, nc.tensor, "pe")
        dve = Lane(nc, ctx, nc.vector, "dve")
        act = Lane(nc, ctx, nc.scalar, "act")
        pool = Lane(nc, ctx, nc.gpsimd, "pool")
        sp = Lane(nc, ctx, nc.sync, "sp")
        lanes = (pe, dve, act, pool, sp)

        def sb(mem, name, shape, dt=F32):
            return mem.enter_context(nc.sbuf_tensor(name, shape, dt))

        def phase(name):
            old = [lane.last for lane in lanes]
            for lane in lanes:
                lane.after(*old)
                lane.phase(name)

        def transfers(name):
            return Transfers(nc, ctx, name)

        ps = ctx.enter_context(nc.psum_tensor("ps", [P, 8, 512], F32))
        x = sb(ctx, "x", [P, B * NT, D])
        ident = sb(ctx, "ident", [P, P])
        ident_bf = sb(ctx, "ident_bf", [P, P], BF16)
        ln_stats = sb(ctx, "ln_stats", [P, NT, 6])
        ln_mv = sb(ctx, "ln_mv", [P, NT, 2])
        ln_var = sb(ctx, "ln_var", [P, NT])
        ln_sd = sb(ctx, "ln_sd", [P, NT])
        ln_r0 = sb(ctx, "ln_r0", [P, NT])
        ln_t = sb(ctx, "ln_t", [P, NT])
        ln_rs = sb(ctx, "ln_rs", [P, NT])
        x_stats = sb(ctx, "x_stats", [P, B * NT, 6])
        x_mv = sb(ctx, "x_mv", [P, B * NT, 2])
        x_var, x_sd, x_r0, x_t, x_rs = (sb(ctx, "x_" + part, [P, B * NT]) for part in ("var", "sd", "r0", "t", "rs"))

        def x_statistics(tile, ready):
            dve.after(ready)
            s = dve.did(nc.vector.bn_stats(x_stats[:, tile, :], x[:, tile, :]))
            dve.after(s)
            return dve.did(nc.vector.bn_aggr(x_mv[:, tile, :], x_stats[:, tile, :]))

        def rsqrt(var, sd, r0, t, rs, ready):
            act.after(ready)
            s = act.did(nc.scalar.activation(sd, var, ACT.Sqrt))
            yield
            dve.after(s)
            s = dve.did(nc.vector.reciprocal(r0, sd))
            dve.after(s)
            s = dve.did(nc.vector.tensor_tensor(t, r0, r0, ALU.mult))
            dve.after(s)
            s = dve.did(nc.vector.scalar_tensor_tensor(t, t, -0.5, var, ALU.mult, ALU.mult))
            dve.after(s)
            dve.did(nc.vector.scalar_tensor_tensor(rs, t, 1.5, r0, ALU.add, ALU.mult))

        def x_rsqrt():
            dve.after(dve.last)
            s = dve.did(nc.vector.tensor_scalar(x_var[:, :], x_mv[:, :, 1], LN_EPS, None, ALU.add))
            for _ in rsqrt(x_var[:, :], x_sd[:, :], x_r0[:, :], x_t[:, :], x_rs[:, :], s):
                pass
            return dve.last

        def x_normed(b, t, z, ready, free):
            i = NT * b + t
            dve.after(ready, free)
            return dve.did(nc.vector.tensor_scalar(z[:, t, :], x[:, i, :], x_mv[:, i, 0:1], x_rs[:, i:i + 1],
                                                   ALU.subtract, ALU.mult))

        def layer_norm(src, dst, ready, free):
            dve.after(ready)
            for t in range(NT):
                s = dve.did(nc.vector.bn_stats(ln_stats[:, t, :], src(t)))
                if t % 2:
                    yield
            dve.after(s)
            for t in range(NT):
                s = dve.did(nc.vector.bn_aggr(ln_mv[:, t, :], ln_stats[:, t, :]))
            dve.after(s)
            s = dve.did(nc.vector.tensor_scalar(ln_var[:, :], ln_mv[:, :, 1], LN_EPS, None, ALU.add))
            yield from rsqrt(ln_var[:, :], ln_sd[:, :], ln_r0[:, :], ln_t[:, :], ln_rs[:, :], s)
            dve.after(dve.last, free)
            for t in range(NT):
                s = dve.did(nc.vector.tensor_scalar(dst(t), src(t), ln_mv[:, t, 0:1], ln_rs[:, t:t + 1],
                                                    ALU.subtract, ALU.mult))
                if t % 2:
                    yield
            return s

        for lane in lanes:
            lane.phase("pair")

        x_in = [transfers(f"x_in{b}") for b in range(B)]
        x_dram = d["x"].rearrange("b (t p) n -> b p t n", p=P)
        for b in range(B):
            x_in[b].start(sp, x[:, NT * b:NT * b + NT, :], x_dram[b])
        s = pool.did(nc.gpsimd.memset(ident[:, :], 0.0))
        pool.after(s)
        s = pool.did(nc.gpsimd.affine_select(out=ident[:, :], in_=ident[:, :], compare_op=ALU.not_equal, fill=1.0,
                                             base=0, pattern=[[-1, P]], channel_multiplier=1))
        pool.after(s)
        ident_ready = pool.did(nc.gpsimd.tensor_copy(ident_bf[:, :], ident[:, :]))

        attn_a = ctx.enter_context(ExitStack())
        v_a = sb(attn_a, "v_a", [P, B, NT, HA, 2])
        qs = sb(attn_a, "qs", [STACK, B, 2, S], F32R)
        ks = sb(attn_a, "ks", [STACK, B, 2, S])
        mask = sb(attn_a, "mask", [P, B * NT, S], BF16)
        own_head = sb(attn_a, "own_head", [STACK, 16])
        wout_t = sb(attn_a, "wout_t", [KA + 1, D])
        small_a = transfers("small_a")
        small_a.start(act, own_head[:, :], d["own_head"])
        small_a.start(act, wout_t[0:KA, :], d["wout_t"])
        small_a.start(act, wout_t[KA:KA + 1, :], d["bout"])

        pair = ctx.enter_context(ExitStack())
        h_neg = sb(pair, "h_neg", [F1, B * S])
        h_b1 = sb(pair, "h_b1", [F1, B * S])
        w2_t = sb(pair, "w2_t", [F1, F2])
        b2_twice = sb(pair, "b2_twice", [P, 1])
        w3_slide = sb(pair, "w3_slide", [P, 62])
        b3_all = sb(pair, "b3_all", [P, 1])
        small_pair = transfers("small_pair")
        small_pair.start(act, w2_t[:, :], d["w2_t"])
        for half in range(2):
            small_pair.start(act, b2_twice[F2 * half:F2 * half + F2, :], d["b2"])
        small_pair.start(act, b3_all[:, :], d["b3"].partition_broadcast(P))
        s = pool.did(nc.gpsimd.memset(w3_slide[:, :], 0.0))
        act.after(s)
        for half in range(2):
            small_pair.start(act, w3_slide[F2 * half:F2 * half + F2, 30 + half:31 + half], d["w3_t"])

        y = sb(pair, "y", [P, NT, D])
        z = sb(pair, "z", [P, NT, D])
        xn_t = sb(pair, "xn_t", [P, ND, S])
        gamma = sb(pair, "gamma", [P, ND])
        beta = sb(pair, "beta", [P, ND])
        w1_t = sb(pair, "w1_t", [P, ND, F1])
        b1 = sb(pair, "b1", [F1, 1])
        wqkv_t = sb(pair, "wqkv_t", [P, ND, 3 * KA])
        b_qk = sb(pair, "b_qk", [P, 1])
        b_v = sb(pair, "b_v", [P, KA])
        qk = sb(pair, "qk", [P, S])
        qk_hi = sb(pair, "qk_hi", [P, S], F32R)
        qk_lo = sb(pair, "qk_lo", [P, S], F32R)
        weights = transfers("weights_a")
        for out, name in ((gamma, "gamma"), (beta, "beta"), (w1_t, "w1_t"), (b1, "b1"), (wqkv_t, "wqkv_t"),
                          (b_qk, "b_qk")):
            weights.start(act, out[:], d[name])
        weights.start(act, b_v[:, :], d["b_v"].partition_broadcast(P))
        pool.after(pool.last)
        q_zero = pool.did(nc.gpsimd.memset(qs[96:STACK, :, :, :].bitcast(F32), 0.0))
        pool.after(q_zero)
        k_one = pool.did(nc.gpsimd.memset(ks[96:STACK, :, :, :], 1.0))

        SIDE_BANKS = (4, 5)
        side_read = {bank: None for bank in SIDE_BANKS}
        n_side = [0]
        y_read, z_read, xn_read, qk_sent = [None], [None], [None], [None]
        stack_dmas = [transfers("stacks_even"), transfers("stacks_odd")]

        def side_bank():
            bank = SIDE_BANKS[n_side[0] % 2]
            n_side[0] += 1
            pe.after(side_read[bank])
            return bank

        def project(b):
            y_ready = yield from layer_norm(lambda t: x[:, NT * b + t, :], lambda t: y[:, t, :], x_in[b].all(),
                                            y_read[0])
            z_ready = yield from layer_norm(lambda t: y[:, t, :], lambda t: z[:, t, :], y_ready, z_read[0])
            pool.after(z_ready, k_one)
            for t in range(NT):
                y_read[0] = pool.did(nc.gpsimd.tensor_tensor(x[:, NT * b + t, :], x[:, NT * b + t, :], y[:, t, :],
                                                             ALU.add))
            pe.after(z_ready, ident_ready)
            act.after(weights.all(), xn_read[0])
            for k in range(ND):
                bank = side_bank()
                for t in range(NT):
                    s = nc.tensor.transpose(ps[:, bank, t * P:t * P + P], z[:, t, k * P:k * P + P], ident[:, :])
                s = z_read[0] = pe.did(s)
                act.after(s)
                xn_ready = side_read[bank] = act.did(nc.scalar.activation(
                    xn_t[:, k, :], ps[:, bank, :], ACT.Identity, bias=beta[:, k:k + 1], scale=gamma[:, k:k + 1]))
                yield
            pe.after(xn_ready, weights.all())
            bank = side_bank()
            for k in range(ND):
                s = nc.tensor.matmul(ps[:, bank, :], w1_t[:, ND - 1 - k, :], xn_t[:, ND - 1 - k, :], start=k == 0,
                                     stop=k == ND - 1)
            s = pe.did(s)
            act.after(s)
            s = act.did(nc.scalar.activation(h_neg[:, b * S:b * S + S], ps[:, bank, :], ACT.Copy, scale=-1.0))
            dve.after(s, weights.all())
            side_read[bank] = h_ready[b] = dve.did(nc.vector.tensor_scalar(h_b1[:, b * S:b * S + S], ps[:, bank, :],
                                                                           b1[:, 0:1], None, ALU.add))
            yield
            bank = side_bank()
            for k in range(ND):
                s = nc.tensor.matmul(ps[:, bank, :], wqkv_t[:, k, 0:2 * KA], xn_t[:, k, :], start=k == 0,
                                     stop=k == ND - 1)
            s = pe.did(s)
            act.after(s)
            s = side_read[bank] = act.did(nc.scalar.activation(qk[:, :], ps[:, bank, :], ACT.Identity,
                                                               bias=b_qk[:, 0:1]))
            yield
            dve.after(s, qk_sent[0])
            s = dve.did(nc.vector.tensor_copy(qk_hi[:, :], qk[:, :]))
            dve.after(s)
            qk_split = dve.did(nc.vector.tensor_tensor(qk_lo[:, :], qk[:, :], qk_hi[:, :].bitcast(F32),
                                                       ALU.subtract))
            sp.after(qk_split)
            for u in range(2):
                for t, (q_src, k_src) in enumerate(((qk_hi, qk_hi), (qk_lo, qk_hi), (qk_hi, qk_lo))):
                    for dst, src, first in ((qs, q_src, 0), (ks, k_src, KA)):
                        at = first + 32 * u
                        qk_sent[0] = stack_dmas[b % 2].start(sp, dst[32 * t:32 * t + 32, b, u, :].bitcast(F32),
                                                             src[at:at + 32, :].bitcast(F32))
            yield
            bank = side_bank()
            for t in range(NT):
                for k in range(ND):
                    s = nc.tensor.matmul(ps[:, bank, t * KA:t * KA + KA], xn_t[:, k, t * P:t * P + P],
                                         wqkv_t[:, k, 2 * KA:3 * KA], start=k == 0, stop=k == ND - 1)
            s = xn_read[0] = pe.did(s)
            dve.after(s)
            for t in range(NT):
                side_read[bank] = dve.did(nc.vector.tensor_tensor(
                    v_a[:, b, t, :, :].rearrange("p h e -> p (h e)"), ps[:, bank, t * KA:t * KA + KA], b_v[:, :],
                    ALU.add))
            yield

        h_ready = [None] * B
        for _ in project(0):
            pass

        with ExitStack() as mem:
            N_PAIR = 16
            pair_in = sb(mem, "pair_in", [F1, N_PAIR, S])
            NG = 4
            pair_mid = sb(mem, "pair_mid", [P, NG, 2, S])
            sim = sb(mem, "sim", [P, 2, S + PAD])
            best = sb(mem, "best", [P, 8])
            in_read = [None] * N_PAIR
            mid_read = [None] * NG
            group_read = [None] * 2
            sim_bank_read = [None] * 2
            sim_free = [None] * 2
            for lane in (pe, act, dve):
                lane.after(small_pair.all())

            def row_of(tile, r, c, half):
                return tile * P + 32 * c + 2 * r + half

            def top_k(tile, sim_ready):
                w = tile % 2
                row = sim[:, w, :]

                def round_(n):
                    def go():
                        dve.after(sim_ready if n == 0 else dve.last)
                        s = dve.did(nc.vector.max(best[:, :], row))
                        dve.after(s)
                        dve.did(nc.vector.match_replace(row, best[:, :], row, TAKEN))
                    return go

                def keep():
                    dve.after(dve.last)
                    sim_free[w] = dve.did(nc.vector.tensor_scalar(mask[:, tile, :], sim[:, w, 0:S], NEVAL, MASKED,
                                                                  ALU.is_gt, ALU.mult))
                return [round_(n) for n in range((TOPK + PAD) // 8)] + [keep]

            rounds = []

            def finish_tile(tile, sims_done):
                w = tile % 2
                act.after(sims_done, sim_free[w])
                s = sim_bank_read[w] = act.did(nc.scalar.activation(sim[:, w, 0:S], ps[:, 6 + w, :], ACT.Identity,
                                                                    bias=b3_all[:, 0:1]))
                pool.after(sim_free[w])
                pool.did(nc.gpsimd.memset(sim[:, w, S:S + PAD], SENTINEL))
                pool.after(s)
                s = pool.did(nc.gpsimd.affine_select(out=sim[:, w, 0:S], in_=sim[:, w, 0:S],
                                                     compare_op=ALU.not_equal, fill=0.0, base=(tile % NT) * P,
                                                     pattern=[[-1, S]], channel_multiplier=1))
                return top_k(tile, s)

            def second_layer(step):
                tile, r, groups = step
                w = tile % 2
                if r == 0:
                    pe.after(sim_bank_read[w])
                for g, (slot, ready) in enumerate(groups):
                    pe.after(ready)
                    for k in range(2):
                        c = 2 * g + k
                        s = nc.tensor.matmul(ps[32 * c:32 * c + 32, 6 + w, :], w3_slide[:, 30 - 2 * r:62 - 2 * r],
                                             pair_mid[:, slot, k, :], start=r == 0, stop=r == 15)
                    mid_read[slot] = s = pe.did(s)
                return s

            behind = None
            n_in = n_group = 0
            projecting = iter(())
            for tile in range(B * NT):
                b = tile // NT
                if tile % NT == 0:
                    for _ in projecting:
                        pass
                    dve.after(h_ready[b])
                    projecting = project(b + 1) if b + 1 < B else iter(())
                for r in range(16):
                    groups = []
                    for g in range(2):
                        slots = []
                        for k in range(2):
                            for half in range(2):
                                i = row_of(tile, r, 2 * g + k, half)
                                slot = n_in % N_PAIR
                                n_in += 1
                                dve.after(in_read[slot])
                                first_ready = dve.did(nc.vector.tensor_scalar(
                                    pair_in[:, slot, :], h_neg[:, b * S:b * S + S], h_b1[:, i:i + 1], 0.0,
                                    ALU.add, ALU.max))
                                slots.append((slot, k, half))
                        bank = 2 * (n_group % 2)
                        pe.after(group_read[n_group % 2], first_ready)
                        for slot, k, half in slots:
                            s = nc.tensor.matmul(ps[F2 * half:F2 * half + F2, bank + k, :], w2_t[:, :],
                                                 pair_in[:, slot, :], start=True, stop=True)
                        s = pe.did(s)
                        for slot, _, _ in slots:
                            in_read[slot] = s
                        mid = n_group % NG
                        act.after(s, mid_read[mid])
                        ready = group_read[n_group % 2] = act.did(nc.scalar.activation(
                            pair_mid[:, mid, :, :], ps[:, bank:bank + 2, :], ACT.Relu, bias=b2_twice[:, 0:1]))
                        groups.append((mid, ready))
                        n_group += 1
                    if behind:
                        s = second_layer(behind)
                        if behind[1] == 15:
                            rounds += finish_tile(behind[0], s)
                    behind = (tile, r, groups)
                    if r % 2 and rounds:
                        rounds.pop(0)()
                    if r % 2 == 0:
                        next(projecting, None)
            s = second_layer(behind)
            rounds += finish_tile(behind[0], s)
            for go in rounds:
                go()

        for lane in lanes:
            lane.after(*(dmas.all() for dmas in stack_dmas))
        pair.close()

        k = Core()
        k.nc, k.d, k.ps, k.x, k.ident, k.ident_bf = nc, d, ps, x, ident, ident_bf
        k.pe, k.dve, k.act, k.pool, k.sp = lanes
        k.sb, k.phase, k.transfers = sb, phase, transfers
        k.x_statistics, k.x_rsqrt, k.x_normed = x_statistics, x_rsqrt, x_normed
        k.v_a, k.qs, k.ks, k.mask, k.own_head, k.wout_t, k.small_a = v_a, qs, ks, mask, own_head, wout_t, small_a
        if upto >= 2:
            attention_a(k)
        attn_a.close()
        out_dram = d["out"].rearrange("b (t p) n -> b p t n", p=P)
        stored = transfers("stored")

        def store(tile, ready):
            sp.after(ready)
            if tile % NT == NT - 1:
                stored.start(sp, out_dram[tile // NT], x[:, tile + 1 - NT:tile + 1, :])

        if upto >= 3:
            feed_forward(k, "ffn1", x_statistics)
        if upto >= 4:
            attention_b(k)
        if upto >= 5:
            feed_forward(k, "ffn2", store)
        else:
            phase("dbg")
            for b in range(B):
                store(NT * b + NT - 1, None)
            if upto == 1:
                stored.start(sp, d["dbg"][0:P, 0:B * NT * S // 2], mask[:, :, :].rearrange("p a b -> p (a b)").bitcast(F32))
        sp.after(stored.all())


def attention_a(k):
    nc, pe, dve, act, pool, sp, ps, x = k.nc, k.pe, k.dve, k.act, k.pool, k.sp, k.ps, k.x
    k.phase("attn_a")
    LEAD, CHUNK, N_KM, N_EX = 18, 16, 3, (6, 8)
    HEADS = B * HA
    with ExitStack() as mem:
        mask_t = k.sb(mem, "mask_t", [P, 2, NT, S], BF16)
        v_aug = k.sb(mem, "v_aug", [P, 2, NT, HA, 3])
        km = k.sb(mem, "km", [STACK, 2 * N_KM, S], F32R)
        ex = k.sb(mem, "ex", [P, sum(N_EX), 2, S])
        maxes = k.sb(mem, "maxes", [P, 2, NT, CHUNK])
        unused = k.sb(mem, "unused", [P, 2, S], BF16)
        max_t = k.sb(mem, "max_t", [CHUNK, 2, S], F32R)
        ao_t = k.sb(mem, "ao_t", [P, 2, HA // 4, S])
        ao = k.sb(mem, "ao", [P, 2, HA, 2])
        r_den = k.sb(mem, "r_den", [P, HA])
        ao_feat = k.sb(mem, "ao_feat", [KA + 1, 2, P])

        OUT_BANK, SIDE_BANK = 6, 7
        pool.after(k.small_a.all())
        s = pool.did(nc.gpsimd.memset(v_aug[:, :, :, :, 2:3], 1.0))
        pool.after(s)
        one_row = pool.did(nc.gpsimd.memset(ao_feat[KA:KA + 1, :, :], 1.0))
        pool.after(one_row)
        bank_zero = dve.did(nc.vector.memset(ps[:, OUT_BANK, :], 0.0))
        pe.after(k.small_a.all(), bank_zero, one_row)
        for lane in (dve, act):
            lane.after(k.small_a.all())

        n_km = [0, 0]
        km_read = [None] * (2 * N_KM)
        o1_read, o2_read = [None] * 2, [None] * 2
        max_read, max_sent = [None] * 2, [None] * 2
        max_dmas = [k.transfers("maxima_even"), k.transfers("maxima_odd")]
        maxes_ready = {}
        in_place = {}
        mask_ready = [None] * B
        mask_read = [None] * B
        v_ready, v_read = [None] * B, [None] * B
        ex_read = [None] * sum(N_EX)
        ao_read = [None] * 2
        side_read = [None]
        counts = {"o1": 0, "group": 0}

        def one_head(engine, kind, n):
            b, u, a = n // HA, n // CHUNK % 2, n % CHUNK
            slot = kind * N_KM + n_km[kind] % N_KM
            n_km[kind] += 1
            engine.after(km_read[slot])
            own = k.own_head[:, a:a + 1]
            if engine is act:
                return slot, act.did(nc.scalar.activation(km[:, slot, :], k.ks[:, b, u, :], ACT.Copy, scale=own))
            return slot, dve.did(nc.vector.tensor_scalar(km[:, slot, :], k.ks[:, b, u, :], own, None, ALU.mult))

        def stack_of(engine, kind, n):
            made = ahead[kind].pop(n, None) or one_head(engine, kind, n)
            if n + 1 < HEADS:
                ahead[kind][n + 1] = one_head(engine, kind, n + 1)
            return made

        ahead = ({}, {})

        def maxima(n):
            b, u, a, w = n // HA, n // CHUNK % 2, n % CHUNK, n // CHUNK % 2
            slot, ready = stack_of(dve, 0, n)
            if a == 0:
                dve.after(max_read[w])
            for t in range(NT):
                bank = counts["o1"] % 2
                counts["o1"] += 1
                pe.after(ready, o1_read[bank])
                s = pe.did(nc.tensor.matmul(ps[:, bank, :], k.qs[:, b, u, t * P:t * P + P], km[:, slot, :],
                                            start=True, stop=True))
                dve.after(s, o1_read[bank])
                o1_read[bank] = dve.did(nc.vector.tensor_tensor_reduce(
                    unused[:, bank, :], ps[:, bank, :], k.mask[:, NT * b + t, :], 1.0, TAKEN, ALU.add, ALU.max,
                    maxes[:, w, t, a:a + 1]))
                km_read[slot] = s
                maxes_ready[n // CHUNK] = o1_read[bank]
                yield

        def place_maxima(chunk):
            b, u, w = chunk // 2, chunk % 2, chunk % 2
            pe.after(maxes_ready[chunk], side_read[0])
            for t in range(NT):
                s = nc.tensor.transpose(ps[0:CHUNK, SIDE_BANK, t * P:t * P + P], maxes[:, w, t, :], k.ident[:, :])
            s = max_read[w] = pe.did(s)
            act.after(s, max_sent[w])
            s = side_read[0] = act.did(nc.scalar.activation(max_t[:, w, :], ps[0:CHUNK, SIDE_BANK, :], ACT.Copy,
                                                            scale=-1.0))
            sp.after(s, km_read[(n_km[0] - 1) % N_KM])
            in_place[chunk] = max_sent[w] = max_dmas[w].start(sp, k.qs[96:STACK, b, u, :].bitcast(F32),
                                                              max_t[:, w, :].bitcast(F32))

        def turn_mask(b, t):
            w = b % 2
            bank = ps[:, SIDE_BANK, 0:S // 2].bitcast(BF16)
            pe.after(side_read[0])
            for i in range(NT):
                s = nc.tensor.transpose(bank[:, i * P:i * P + P], k.mask[:, NT * b + i, t * P:t * P + P],
                                        k.ident_bf[:, :])
            s = pe.did(s)
            act.after(s, mask_read[b - 2] if b >= 2 else None)
            mask_ready[b] = side_read[0] = act.did(nc.scalar.activation(mask_t[:, w, t, :], bank, ACT.Copy))

        def values(b):
            w = b % 2
            pool.after(v_read[b - 2] if b >= 2 else None)
            v_ready[b] = pool.did(nc.gpsimd.tensor_copy(
                v_aug[:, w, :, :, 0:2].rearrange("p t h e -> p (t h) e"),
                k.v_a[:, b, :, :, :].rearrange("p t h e -> p (t h) e")))

        def exponentials(n, out):
            b, u, w = n // HA, n // CHUNK % 2, (n // HA) % 2
            slot, ready = stack_of(act, 1, n)
            pe.after(ready, in_place[n // CHUNK], mask_ready[b])
            for g in range(NT // 2):
                pair_of_banks, e = counts["group"] % 2, g * N_EX[0] + n % N_EX[g]
                counts["group"] += 1
                bank = 2 + 2 * pair_of_banks
                pe.after(o2_read[pair_of_banks])
                for j in range(2):
                    t = 2 * g + j
                    nc.tensor.matmul(ps[:, bank + j, :], k.ident_bf[:, :], mask_t[:, w, t, :], start=True, stop=False)
                    s = nc.tensor.matmul(ps[:, bank + j, :], km[:, slot, t * P:t * P + P], k.qs[:, b, u, :],
                                         start=False, stop=True)
                s = pe.did(s)
                act.after(s, ex_read[e])
                s2 = o2_read[pair_of_banks] = act.did(nc.scalar.activation(ex[:, e, :, :], ps[:, bank:bank + 2, :], ACT.Exp,
                                                                           scale=2.0 ** -0.5))
                out.append((e, s2))
                km_read[slot] = s
                mask_read[b] = s
                yield

        def weighted(n, groups):
            b, w, block = n // HA, (n // HA) % 2, n % HA // 4
            pe.after(v_ready[b], out_read[0])
            for t in range(NT):
                for g in range(4):
                    e, ready = groups[g][t // 2]
                    pe.after(ready)
                    s = nc.tensor.matmul(ps[32 * g:32 * g + 3, OUT_BANK, :], v_aug[:, w, t, 4 * block + g, :],
                                         ex[:, e, t % 2, :], start=t == 0, stop=t == NT - 1)
                s = pe.did(s)
                for g in groups:
                    ex_read[g[t // 2][0]] = s
                if t < NT - 1:
                    yield
            v_read[b] = s
            act.after(s, ao_read[w] if block == 0 else None)
            s = out_read[0] = act.did(nc.scalar.activation(ao_t[:, w, block, :], ps[:, OUT_BANK, :], ACT.Copy))
            if block == HA // 4 - 1:
                side[:0] = finish(b, s)
            yield

        out_read = [bank_zero]

        def finish(b, ao_ready):
            w = b % 2
            steps = []
            for t in range(NT):
                for half in range(2):
                    def divide(t=t, half=half):
                        pe.after(ao_ready, side_read[0])
                        for i in range(4):
                            s = nc.tensor.transpose(ps[:, SIDE_BANK, i * P:i * P + P],
                                                    ao_t[:, w, 4 * half + i, t * P:t * P + P], k.ident[:, :])
                        s = pe.did(s)
                        ao_read[w] = s
                        sums = ps[:, SIDE_BANK, :].rearrange("p (h r) -> p h r", r=32)
                        part = r_den[:, 16 * half:16 * half + 16]
                        dve.after(s)
                        s = dve.did(nc.vector.reciprocal(part, sums[:, :, 2]))
                        dve.after(s)
                        for e in range(2):
                            s = dve.did(nc.vector.tensor_tensor(ao[:, t % 2, 16 * half:16 * half + 16, e], sums[:, :, e],
                                                                part, ALU.mult))
                        side_read[0] = k.ao_done = s
                    steps.append(divide)

                def turn(t=t):
                    pe.after(k.ao_done, side_read[0])
                    s = pe.did(nc.tensor.transpose(ps[0:KA, SIDE_BANK, 0:P],
                                                   ao[:, t % 2, :, :].rearrange("p h e -> p (h e)"), k.ident[:, :]))
                    act.after(s)
                    side_read[0] = k.feat_done = act.did(nc.scalar.activation(ao_feat[0:KA, t % 2, :],
                                                                              ps[0:KA, SIDE_BANK, 0:P], ACT.Copy))
                steps.append(turn)

                def project(t=t):
                    pe.after(k.feat_done, side_read[0])
                    s = pe.did(nc.tensor.matmul(ps[:, SIDE_BANK, :], ao_feat[:, t % 2, :], k.wout_t[:, :], start=True,
                                                stop=True))
                    dve.after(s)
                    side_read[0] = dve.did(nc.vector.tensor_tensor(x[:, NT * b + t, :], x[:, NT * b + t, :],
                                                                   ps[:, SIDE_BANK, :], ALU.add))
                    k.x_statistics(NT * b + t, side_read[0])
                steps.append(project)
            return steps

        side = []
        values(0)
        for t in range(NT):
            turn_mask(0, t)
        for n in range(LEAD):
            for _ in maxima(n):
                pass
            if n == CHUNK:
                place_maxima(0)
        groups = []
        behind = iter(())
        for n in range(HEADS + 4):
            b, h = n // HA, n % HA
            if h == 4 and b + 1 < B:
                values(b + 1)
                side += [lambda t=t, b=b: turn_mask(b + 1, t) for t in range(NT)]
            groups.append([])
            ahead_steps = maxima(n + LEAD) if n + LEAD < HEADS else iter(())
            own_steps = exponentials(n, groups[-1]) if n < HEADS else iter(())
            for steps in (own_steps, ahead_steps, behind, ahead_steps, own_steps, ahead_steps):
                next(steps, None)
            if side:
                side.pop(0)()
            for _ in ahead_steps:
                pass
            next(own_steps, None)
            if (n + LEAD) % CHUNK == 0 and n + LEAD <= HEADS:
                place_maxima((n + LEAD) // CHUNK - 1)
            if h % 4 == 3:
                behind, groups = weighted(n - 3, groups), []
        for step in side:
            step()


def feed_forward(k, name, tile_done):
    nc, pe, dve, act, pool, sp, ps, x = k.nc, k.pe, k.dve, k.act, k.pool, k.sp, k.ps, k.x
    k.phase(name)
    OC = 2
    CHUNKS = NI // OC
    WU, WD = ND * 2 * OC * P, OC * D
    with ExitStack() as mem:
        raw = k.sb(mem, name + "_raw", [P, 2, WU + WD])
        w_hi = k.sb(mem, name + "_w_hi", [P, 2, WU + WD], F32R)
        w_lo = k.sb(mem, name + "_w_lo", [P, 2, WU + WD], F32R)
        z = k.sb(mem, name + "_z", [P, NT, D])
        z_hi = k.sb(mem, name + "_z_hi", [P, ND, B * S], F32R)
        z_lo = k.sb(mem, name + "_z_lo", [P, ND, B * S], F32R)
        silu = k.sb(mem, name + "_silu", [P, 2, S])
        inner = k.sb(mem, name + "_inner", [P, 2, S])
        in_hi = k.sb(mem, name + "_in_hi", [P, 2, OC, S], F32R)
        in_lo = k.sb(mem, name + "_in_lo", [P, 2, OC, S], F32R)
        loads = [k.transfers(f"{name}_w{i}") for i in range(2)]
        w_read = [None] * 2
        raw_read = [[], []]
        w_ready = {}
        z_ready, z_free = {}, None
        bank_read = [None] * 8
        silu_read, in_read = [None] * 2, [None] * 2

        def load(c):
            w = c % 2
            sp.after(*raw_read[w])
            return loads[w].start(sp, raw[:, w, :], k.d["w_ffn"][c])

        def split(c, arrived):
            w = c % 2
            act.after(arrived, w_read[w])
            w_ready[c] = []
            for a, e in ((0, WU // 2), (WU // 2, WU), (WU, WU + WD)):
                s = act.did(nc.scalar.activation(w_hi[:, w, a:e], raw[:, w, a:e], ACT.Copy))
                pool.after(s)
                s = pool.did(nc.gpsimd.tensor_tensor(w_lo[:, w, a:e], raw[:, w, a:e], w_hi[:, w, a:e].bitcast(F32),
                                                     ALU.subtract))
                w_ready[c].append(s)
            raw_read[w] = [s]

        def normed(b):
            for t in range(NT):
                s = k.x_normed(b, t, z, rs_ready, z_read[0])
            yield
            pe.after(s)
            for f in range(ND):
                bank = 6 + f % 2
                pe.after(bank_read[bank])
                for t in range(NT):
                    s = nc.tensor.transpose(ps[:, bank, t * P:t * P + P], z[:, t, f * P:f * P + P], k.ident[:, :])
                s = z_read[0] = pe.did(s)
                act.after(s)
                at = slice(b * S, b * S + S)
                s = act.did(nc.scalar.activation(z_hi[:, f, at], ps[:, bank, :], ACT.Copy))
                dve.after(s)
                bank_read[bank] = z_ready[b] = dve.did(nc.vector.tensor_tensor(
                    z_lo[:, f, at], ps[:, bank, :], z_hi[:, f, at].bitcast(F32), ALU.subtract))
                if f % 2:
                    yield

        def up(c, b, o):
            w = c % 2
            for g in range(2):
                bank = 2 * (o % 2) + g
                pe.after(bank_read[bank])
                n = 0
                for z_part, w_part in ((z_hi, w_hi), (z_lo, w_hi), (z_hi, w_lo)):
                    for f in range(ND):
                        at = (f * 2 + g) * OC * P + o * P
                        s = nc.tensor.matmul(ps[:, bank, :], w_part[:, w, at:at + P], z_part[:, f, b * S:b * S + S],
                                             start=n == 0, stop=n == 3 * ND - 1)
                        n += 1
                s = pe.did(s)
                if g == 0:
                    act.after(s, silu_read[o % 2])
                    gate = bank_read[bank] = act.did(nc.scalar.activation(silu[:, o % 2, :], ps[:, bank, :], ACT.Silu))
            u = (c * B + b) % 2
            dve.after(s, gate)
            s = silu_read[o % 2] = bank_read[bank] = dve.did(nc.vector.tensor_tensor(
                inner[:, o % 2, :], silu[:, o % 2, :], ps[:, bank, :], ALU.mult))
            dve.after(s, in_read[u])
            s = dve.did(nc.vector.tensor_copy(in_hi[:, u, o, :], inner[:, o % 2, :]))
            dve.after(s)
            return dve.did(nc.vector.tensor_tensor(in_lo[:, u, o, :], inner[:, o % 2, :], in_hi[:, u, o, :].bitcast(F32),
                                                   ALU.subtract))

        def down(c, b, t, ready):
            w, u = c % 2, (c * B + b) % 2
            bank = 4 + t % 2
            pe.after(ready, w_ready[c][2], bank_read[bank])
            n = 0
            for i_part, w_part in ((in_hi, w_hi), (in_lo, w_hi), (in_hi, w_lo)):
                for o in range(OC):
                    s = nc.tensor.matmul(ps[:, bank, :], i_part[:, u, o, t * P:t * P + P],
                                         w_part[:, w, WU + o * D:WU + o * D + D], start=n == 0, stop=n == 3 * OC - 1)
                    n += 1
            s = pe.did(s)
            in_read[u] = s
            if b == B - 1:
                w_read[w] = s
            dve.after(s, x_done[b])
            bank_read[bank] = dve.did(nc.vector.tensor_tensor(x[:, NT * b + t, :], x[:, NT * b + t, :], ps[:, bank, :],
                                                              ALU.add))
            if c == CHUNKS - 1:
                tile_done(NT * b + t, bank_read[bank])
            return bank_read[bank]

        z_read = [None]
        x_done = [None] * B
        arrived = [load(0), load(1)]
        rs_ready = k.x_rsqrt()
        split(0, arrived[0])
        for _ in normed(0):
            pass
        behind = None
        for c in range(CHUNKS):
            for b in range(B):
                pe.after(w_ready[c][1], z_ready[b])
                norm = normed(b + 1) if c == 0 and b + 1 < B else iter(())
                next(norm, None)
                for o in range(OC):
                    s = up(c, b, o)
                    next(norm, None)
                    if behind:
                        for t in range(2 * o, 2 * o + 2):
                            s_x = down(*behind[:2], t, behind[2])
                        if o == OC - 1:
                            x_done[behind[1]] = s_x
                behind = (c, b, s)
                for _ in norm:
                    pass
                if b == 0 and c + 1 < CHUNKS:
                    split(c + 1, arrived[(c + 1) % 2])
                    if c + 2 < CHUNKS:
                        arrived[c % 2] = load(c + 2)
        for t in range(NT):
            down(*behind[:2], t, behind[2])


def attention_b(k):
    nc, pe, dve, act, pool, sp, ps, x, d = k.nc, k.pe, k.dve, k.act, k.pool, k.sp, k.ps, k.x, k.d
    k.phase("attn_b")
    ROWS, N_EX, HU, SCALE = 97, 10, 4, HDB ** -0.5
    UNITS = B * (HB // HU)
    with ExitStack() as mem:
        w_qk = k.sb(mem, "wb_qk", [P, ND, HB // HU, 2, P])
        w_v = k.sb(mem, "wb_v", [P, ND, D])
        w_proj = k.sb(mem, "wb_proj", [P, ND, D])
        z = k.sb(mem, "zb", [P, NT, D])
        z_t = k.sb(mem, "zb_t", [P, 2, ND, S])
        hi = k.sb(mem, "hi_b", [P, 2, S], F32R)
        lo = k.sb(mem, "lo_b", [P, 2, S], F32R)
        q_stack = k.sb(mem, "q_stack", [ROWS, 3, HU, S], F32R)
        k_stack = k.sb(mem, "k_stack", [ROWS, 3, HU, S], F32R)
        v = k.sb(mem, "vb", [P, 2, NT, D])
        ex = k.sb(mem, "ex_b", [P, N_EX, S])
        ex_sum = k.sb(mem, "ex_sum", [P, HU, S])
        out_t = k.sb(mem, "out_t", [P, ND, S])
        sums_sb = k.sb(mem, "sums_sb", [P, 2, S])
        maxes = k.sb(mem, "maxes_b", [P, 2, HU, NT])
        max_t = k.sb(mem, "max_t_b", [HU, 2, S], F32R)
        ones = k.sb(mem, "ones_b", [P, 32])
        lam_in = ex[0:1, 0:4, :]
        lam_unused = ex[0:1, 4:6, :]
        lam = k.sb(mem, "lam", [1, 4])
        q2_row = k.sb(mem, "q2_row", [1, P])
        q1_col = k.sb(mem, "q1_col", [P, 1])
        q_scale = k.sb(mem, "q_scale", [P, 1])

        halves = nc.dram_tensor("halves", (2, 2, P, 2, S), F32).ap()
        halves_dmas = [k.transfers("halves_even"), k.transfers("halves_odd")]

        O2_BANKS, SUM_BANK, SIDE_BANKS = (2, 3, 4), 5, (6, 7)
        rs_ready = k.x_rsqrt()
        small = k.transfers("small_b")
        small.start(sp, lam_in[:, :, :], d["lambdas"])
        small.start(sp, q2_row[:, :], d["q2_row"])
        small.start(sp, q1_col[:, :], d["q1_col"])
        qk_weights, v_weights, proj_weights = (k.transfers(f"weights_b_{part}") for part in ("qk", "v", "proj"))
        qk_weights.start(sp, w_qk[:, :, :, :, :], d["wb_qk"])

        s = pool.did(nc.gpsimd.memset(ones[:, :], 1.0))
        pool.after(s)
        s = pool.did(nc.gpsimd.memset(k_stack[96:97, :, :, :].bitcast(F32), 1.0))
        ones_ready = s

        side_read = {bank: None for bank in SIDE_BANKS}
        q_scale_ready = [None]
        n_side = [0]
        z_read, z_ready, z_t_read, z_t_ready = [None], [None], [None] * B, [None] * B
        o1_read, o2_read = [None] * 2, [None] * 3
        ex_read, added = [None] * N_EX, [None] * N_EX
        v_ready, v_read = [None] * B, [None] * B
        sum_read, out_read, ex_sum_read, sums_free = [ones_ready], [None], [None], [None]
        product_done = [[None] * 2 for _ in range(UNITS)]
        stack_dmas = [k.transfers(f"stacks_b{i}") for i in range(3)]
        max_dmas = [k.transfers("maxima_b_even"), k.transfers("maxima_b_odd")]
        stacked, hi_sent = [None] * UNITS, [None]
        in_place = [None] * UNITS
        max_ready, o2_last = [None] * UNITS, [None] * UNITS
        max_read = [None] * 2
        ex_sum_ready = [None] * HU
        n_o2 = [0]

        def query_scale():
            dve.after(small.all())
            for i in range(2):
                s = dve.did(nc.vector.tensor_tensor_reduce(lam_unused[:, i, :], lam_in[:, 2 * i, :], lam_in[:, 2 * i + 1, :],
                                                           1.0, 0.0, ALU.mult, ALU.add, lam[:, i:i + 1]))
            act.after(s)
            s = act.did(nc.scalar.activation(lam[:, 2:4], lam[:, 0:2], ACT.Exp))
            dve.after(s)
            s = dve.did(nc.vector.tensor_tensor(lam[:, 0:1], lam[:, 3:4], lam[:, 2:3], ALU.subtract))
            dve.after(s)
            s = dve.did(nc.vector.tensor_scalar(lam[:, 1:2], lam[:, 0:1], -LAMBDA_INIT, None, ALU.add))
            pe.after(s, side_read[SIDE_BANKS[0]])
            s = pe.did(nc.tensor.matmul(ps[:, SIDE_BANKS[0], 0:1], q2_row[:, :], lam[:, 1:2], start=True, stop=True))
            dve.after(s)
            q_scale_ready[0] = side_read[SIDE_BANKS[0]] = dve.did(nc.vector.tensor_tensor(q_scale[:, :], ps[:, SIDE_BANKS[0], 0:1], q1_col[:, :], ALU.add))

        def side_bank():
            bank = SIDE_BANKS[n_side[0] % 2]
            n_side[0] += 1
            pe.after(side_read[bank])
            return bank

        def norm_steps(b):
            def norm(t):
                z_ready[0] = k.x_normed(b, t, z, rs_ready, z_read[0])
            light[:0] = [lambda t=t: norm(t) for t in range(NT)]
            steps = []
            for f in range(ND):
                def turn(f=f):
                    pe.after(z_ready[0])
                    bank = side_bank()
                    for t in range(NT):
                        s = nc.tensor.transpose(ps[:, bank, t * P:t * P + P], z[:, t, f * P:f * P + P], k.ident[:, :])
                    s = z_read[0] = pe.did(s)
                    act.after(s, z_t_read[b - 2] if b >= 2 else None)
                    side_read[bank] = z_t_ready[b] = act.did(nc.scalar.activation(z_t[:, b % 2, f, :], ps[:, bank, :],
                                                                                  ACT.Copy))
                steps.append(turn)
            for t in range(NT):
                def values(t=t):
                    pe.after(z_t_ready[b], v_weights.all())
                    bank = side_bank()
                    for f in range(ND):
                        s = nc.tensor.matmul(ps[:, bank, :], z_t[:, b % 2, f, t * P:t * P + P], w_v[:, f, :],
                                             start=f == 0, stop=f == ND - 1)
                        if f == ND // 2 - 1:
                            yield
                    s = pe.did(s)
                    act.after(s, v_read[b - 2] if b >= 2 else None)
                    side_read[bank] = v_ready[b] = act.did(nc.scalar.activation(v[:, b % 2, t, :], ps[:, bank, :],
                                                                                ACT.Copy))
                steps.append(values)
            return steps

        def query_key_steps(n):
            b, c, w = n // (HB // HU), n % (HB // HU), n % 3
            steps = []
            for i in range(2):
                def product(i=i):
                    pe.after(z_t_ready[b], qk_weights.all())
                    bank = side_bank()
                    for f in range(ND):
                        s = nc.tensor.matmul(ps[:, bank, :], w_qk[:, f, c, i, :], z_t[:, b % 2, f, :], start=f == 0,
                                             stop=f == ND - 1)
                        if f == ND // 2 - 1:
                            yield
                    s = pe.did(s)
                    z_t_read[b] = s
                    act.after(s, hi_sent[0], q_scale_ready[0])
                    scale = 1.0 if i else q_scale[:, 0:1]
                    s = act.did(nc.scalar.activation(hi[:, i, :], ps[:, bank, :], ACT.Copy, scale=scale))
                    dve.after(s)
                    side_read[bank] = product_done[n][i] = dve.did(nc.vector.scalar_tensor_tensor(
                        lo[:, i, :], ps[:, bank, :], scale, hi[:, i, :].bitcast(F32), ALU.mult, ALU.subtract))
                steps.append(product)

            def send():
                sp.after(*product_done[n], o2_last[n - 3] if n >= 3 else None, ones_ready)
                for half, part in enumerate((hi, lo)):
                    sent = halves_dmas[n % 2].start(sp, halves[n % 2, half], part[:, :, :].bitcast(F32))
                sp.after(sent)
                for r, (q_half, k_half) in enumerate(((0, 0), (1, 0), (0, 1))):
                    for stack, half, i in ((q_stack, q_half, 0), (k_stack, k_half, 1)):
                        stacked[n] = stack_dmas[w].start(sp, stack[32 * r:32 * r + 32, w, :, :].bitcast(F32),
                                                         halves[n % 2, half, :, i, :].rearrange("(g p) s -> p g s", g=HU))
                hi_sent[0] = sent
            return steps + [send]

        def maxima(n):
            w, s3 = n % 2, n % 3
            pe.after(stacked[n])
            dve.after(max_read[w])
            for i in range(HU * NT):
                g, t = i // NT, i % NT
                pe.after(o1_read[i % 2])
                s = pe.did(nc.tensor.matmul(ps[:, i % 2, :], q_stack[0:ROWS - 1, s3, g, t * P:t * P + P],
                                            k_stack[0:ROWS - 1, s3, g, :], start=True, stop=True))
                dve.after(s)
                o1_read[i % 2] = dve.did(nc.vector.tensor_reduce(maxes[:, w, g, t:t + 1], ps[:, i % 2, :], AX.X, ALU.max))
                max_ready[n] = o1_read[i % 2]
                yield

        def place_maxima(n):
            w = n % 2
            pe.after(max_ready[n])
            bank = side_bank()
            for t in range(NT):
                s = nc.tensor.transpose(ps[0:HU, bank, t * P:t * P + P], maxes[:, w, :, t], k.ident[:, :])
            s = max_read[w] = pe.did(s)
            act.after(s, in_place[n - 2] if n >= 2 else None)
            s = side_read[bank] = act.did(nc.scalar.activation(max_t[:, w, :], ps[0:HU, bank, :], ACT.Copy, scale=-1.0))
            act.after(s, o2_last[n - 3] if n >= 3 else None)
            for g in range(HU):
                in_place[n] = max_dmas[w].start(act, q_stack[ROWS - 1:ROWS, n % 3, g, :].bitcast(F32),
                                                max_t[g:g + 1, w, :].bitcast(F32))

        def exponentials(n, tiles):
            w = n % 3
            pe.after(in_place[n])
            for t in range(NT):
                for g in range(HU):
                    o, e = n_o2[0] % 3, n_o2[0] % N_EX
                    n_o2[0] += 1
                    bank = O2_BANKS[o]
                    pe.after(o2_read[o])
                    s = o2_last[n] = pe.did(nc.tensor.matmul(ps[:, bank, :], k_stack[:, w, g, t * P:t * P + P],
                                                             q_stack[:, w, g, :], start=True, stop=True))
                    act.after(s, ex_read[e], added[e])
                    s = o2_read[o] = act.did(nc.scalar.activation(ex[:, e, :], ps[:, bank, :], ACT.Exp, scale=SCALE))
                    tiles.append((e, s))
                    pool.after(s, ex_sum_read[0] if t == 1 else None)
                    if t > 0:
                        first = ex[:, tiles[g][0], :] if t == 1 else ex_sum[:, g, :]
                        pool.after(ex_sum_ready[g])
                        s = ex_sum_ready[g] = pool.did(nc.gpsimd.tensor_tensor(ex_sum[:, g, :], first, ex[:, e, :],
                                                                               ALU.add))
                        if t == 1:
                            added[tiles[g][0]] = s
                        added[e] = s
                    yield

        def weighted(n, tiles):
            b, c = n // (HB // HU), n % (HB // HU)
            pe.after(v_ready[b], sum_read[0])
            for t in range(NT):
                for g in range(HU):
                    e, ready = tiles[HU * t + g]
                    pe.after(ready)
                    at = P * c + 32 * g
                    s = nc.tensor.matmul(ps[32 * g:32 * g + 32, SUM_BANK, :], v[:, b % 2, t, at:at + 32], ex[:, e, :],
                                         start=t == 0, stop=t == NT - 1)
                s = pe.did(s)
                for g in range(HU):
                    ex_read[tiles[HU * t + g][0]] = s
                if t < NT - 1:
                    yield
            v_read[b] = s
            act.after(s, sums_free[0])
            sum_read[0] = act.did(nc.scalar.activation(sums_sb[:, 0, :], ps[:, SUM_BANK, :], ACT.Copy))
            ready = list(ex_sum_ready)

            def denominators():
                pe.after(*ready)
                bank = side_bank()
                for g in range(HU):
                    s = nc.tensor.matmul(ps[32 * g:32 * g + 32, bank, :], ones[:, :], ex_sum[:, g, :], start=True,
                                         stop=True)
                s = ex_sum_read[0] = pe.did(s)
                act.after(s)
                s = side_read[bank] = act.did(nc.scalar.activation(sums_sb[:, 1, :], ps[:, bank, :], ACT.Copy))
                light.extend(divide_steps(b, c, s))
            side.insert(0, denominators)
            yield

        def divide_steps(b, c, ready):
            steps = []
            for piece in range(2 * NT):
                def go(piece=piece):
                    t, at = piece // 2, slice(piece * P // 2, piece * P // 2 + P // 2)
                    dve.after(ready, out_read[0])
                    s = dve.did(nc.vector.reciprocal(sums_sb[:, 1, at], sums_sb[:, 1, at]))
                    dve.after(s)
                    s = sums_free[0] = dve.did(nc.vector.tensor_tensor(out_t[:, c, at], sums_sb[:, 0, at],
                                                                       sums_sb[:, 1, at], ALU.mult))
                    if c == HB // HU - 1 and piece % 2:
                        side.append(project_step(b, t, s))
                steps.append(go)
            return steps

        def project_step(b, t, ready):
            def go():
                pe.after(ready, proj_weights.all())
                bank = side_bank()
                for c in range(ND):
                    s = nc.tensor.matmul(ps[:, bank, :], out_t[:, c, t * P:t * P + P], w_proj[:, c, :],
                                         start=c == 0, stop=c == ND - 1)
                    if c == ND // 2 - 1:
                        yield
                s = out_read[0] = pe.did(s)
                dve.after(s)
                side_read[bank] = dve.did(nc.vector.scalar_tensor_tensor(
                    x[:, NT * b + t, :], ps[:, bank, :], 1.0 - LAMBDA_INIT, x[:, NT * b + t, :], ALU.mult,
                    ALU.add))
                k.x_statistics(NT * b + t, side_read[bank])
            return go

        TILES, LAG = HU * NT, 6
        UNITS_B = HB // HU
        side, light = [], []
        due = []
        half_done = []

        def advance():
            step = half_done.pop() if half_done else side.pop(0)()
            if step and next(step, "done") is None:
                half_done.append(step)

        due = norm_steps(0)
        side += due[:ND] + query_key_steps(0)
        due = due[ND:]
        for step in light:
            step()
        light.clear()
        query_scale()
        while side or half_done:
            advance()
        v_weights.start(sp, w_v[:, :, :], d["wb_v"])
        proj_weights.start(sp, w_proj[:, :, :], d["wb_proj"])
        tiles = {}
        rows, own, sums = iter(()), iter(()), iter(())
        for m in range(TILES * (UNITS + 1) + LAG + HU + 4):
            n, i = m // TILES, m % TILES
            if i == 0 and n < UNITS:
                rows = maxima(n)
                if n % UNITS_B == 0 and n // UNITS_B + 1 < B:
                    due += norm_steps(n // UNITS_B + 1)
                share = (ND + (NT if n == 0 else 0), 0, NT // 2, NT // 2)[n % UNITS_B]
                query_key = query_key_steps(n + 1) if n + 1 < UNITS else []
                side = query_key[:2] + side + due[:share]
                due = due[share:]
            if i == LAG + 1:
                side[:0] = query_key[2:]
                query_key = []
            if i == LAG and 1 <= n <= UNITS:
                tiles[n - 1] = []
                own = exponentials(n - 1, tiles[n - 1])
            if i == (LAG + HU) % TILES and 1 <= n <= UNITS:
                sums = weighted(n - 1, tiles[n - 1])
            next(own, None)
            if i == 0 and 1 <= n <= UNITS:
                place_maxima(n - 1)
            next(rows, None)
            if (i - LAG - HU) % HU == 0:
                next(sums, None)
            if side or half_done:
                advance()
            if light:
                light.pop(0)()
        while side or light or half_done:
            if light:
                light.pop(0)()
            else:
                advance()


def layout(inputs):
    import numpy as np

    def of(name):
        return np.asarray(inputs["L0_" + name])

    def feature_major(w):
        return w.T.reshape(ND, P, -1).transpose(1, 0, 2)

    a = {"x": of("attn_a_x")}
    a["gamma"] = of("attn_a_gamma").reshape(ND, P).T
    a["beta"] = of("attn_a_beta").reshape(ND, P).T
    a["w1_t"] = feature_major(of("attn_a_W1"))
    a["b1"] = of("attn_a_b1")[:, None]
    a["w2_t"] = of("attn_a_W2").T
    a["b2"] = of("attn_a_b2")[:, None]
    a["w3_t"] = of("attn_a_W3").T
    a["b3"] = of("attn_a_b3")
    a["wqkv_t"] = feature_major(of("attn_a_Wqkv"))
    a["b_qk"] = of("attn_a_bqkv")[:2 * KA, None]
    a["b_v"] = of("attn_a_bqkv")[2 * KA:]
    a["wout_t"] = of("attn_a_Wout").T
    a["bout"] = of("attn_a_bout")[None]
    one = np.eye(16, dtype=np.float32)
    a["own_head"] = np.concatenate([np.repeat(one, 2, axis=0)] * (HALVES // 2) + [one])

    oc, chunks = 2, NI // 2
    up = of("ffn_w_gate_up").reshape(2, chunks, oc, P, ND, P).transpose(1, 5, 4, 0, 2, 3).reshape(chunks, P, -1)
    down = of("ffn_w_down").T.reshape(chunks, oc, P, D).transpose(0, 2, 1, 3).reshape(chunks, P, -1)
    a["w_ffn"] = np.concatenate([up, down], axis=-1)

    w = of("attn_b_W_attn").reshape(ND, P, 3 * D).transpose(1, 0, 2)
    q1, k1, q2, k2 = (w[:, :, i * D // 2:(i + 1) * D // 2].reshape(P, ND, HB // 4, 4, HDB) for i in range(4))
    q = np.stack([q1, q2], axis=4).reshape(P, ND, HB // 4, P)
    k = np.stack([k1, k2], axis=4).reshape(P, ND, HB // 4, P)
    a["wb_qk"] = np.stack([q, k], axis=3)
    a["wb_v"] = w[:, :, 2 * D:]
    a["wb_proj"] = of("attn_b_W_proj").reshape(ND, P, D).transpose(1, 0, 2)
    a["lambdas"] = np.stack([of("attn_b_lambda_" + n) for n in ("q1", "k1", "q2", "k2")])[None]
    second = (np.arange(P) // HDB % 2).astype(np.float32)
    a["q2_row"] = second[None]
    a["q1_col"] = (np.arange(P) // HDB % 2 == 0).astype(np.float32)[:, None]
    return {name: np.ascontiguousarray(v) for name, v in a.items()}


def kernel(**inputs):
    import concourse.bacc as bacc
    from concourse.bass_utils import run_bass_kernel_spmd

    arrays = {"in_" + name: v for name, v in layout(inputs).items()}
    nc = bacc.Bacc("TRN2", target_bir_lowering=False, num_devices=1)
    d = {name[3:]: nc.dram_tensor(name, v.shape, mybir.dt.from_np(v.dtype), kind="ExternalInput").ap()
         for name, v in arrays.items()}
    d["out"] = nc.dram_tensor("out", (B, S, D), F32, kind="ExternalOutput").ap()
    build(nc, d)
    return run_bass_kernel_spmd(nc, [arrays], core_ids=[0]).results[0]["out"]
```

```python
from contextlib import ExitStack

import concourse.bass as bass
from concourse import mybir

ALU = mybir.AluOpType
ACT = mybir.ActivationFunctionType
AX = mybir.AxisListType
F32 = mybir.dt.float32
F32R = mybir.dt.float32r
BF16 = mybir.dt.bfloat16

P = 128
B, S, D = 4, 512, 512
NT = S // P
ND = D // P
F1, F2 = 128, 64
TOPK = max(1, int(S * 0.1))
HA, KA = 32, 64
HB, HDB = 16, 16
INTER = 2048
NI = INTER // P
LN_EPS = 1e-5
LAMBDA_INIT = 0.8 - 0.6 * 1.0
MASKED = -1e30
TAKEN = -3e38
SENTINEL = 3e38
KEPT_ABOVE = -2.9e38
PAD = (-TOPK) % 8
HALVES = 6
STACK = 16 * (HALVES + 1)


class Lane:

    def __init__(self, nc, ctx, engine, name):
        self.nc, self.ctx, self.engine, self.name = nc, ctx, engine, name
        self.waited = {}
        self.last = None

    def phase(self, name):
        self.sem_name = f"{self.name}_{name}"
        self.sem = self.ctx.enter_context(self.nc.semaphore(self.sem_name))
        self.count = 0

    def did(self, instruction):
        self.count += 1
        instruction.then_inc(self.sem, 1)
        self.last = (self.sem_name, self.sem, self.count)
        return self.last

    def after(self, *signals):
        for signal in signals:
            if signal is None:
                continue
            name, sem, value = signal
            if self.waited.get(name, 0) < value:
                self.engine.wait_ge(sem, value)
                self.waited[name] = value


class Transfers:

    def __init__(self, nc, ctx, name):
        self.name, self.sem, self.count = name, ctx.enter_context(nc.semaphore(name)), 0

    def start(self, lane, out, in_):
        self.count += 16
        lane.engine.dma_start(out, in_).then_inc(self.sem, 16)
        return self.all()

    def all(self):
        return (self.name, self.sem, self.count)


class Core:
    pass


def build(nc, d):
    with ExitStack() as ctx:
        pe = Lane(nc, ctx, nc.tensor, "pe")
        dve = Lane(nc, ctx, nc.vector, "dve")
        act = Lane(nc, ctx, nc.scalar, "act")
        pool = Lane(nc, ctx, nc.gpsimd, "pool")
        sp = Lane(nc, ctx, nc.sync, "sp")
        lanes = (pe, dve, act, pool, sp)

        def sb(mem, name, shape, dt=F32):
            return mem.enter_context(nc.sbuf_tensor(name, shape, dt))

        def phase(name):
            old = [lane.last for lane in lanes]
            for lane in lanes:
                lane.after(*old)
                lane.phase(name)

        def transfers(name):
            return Transfers(nc, ctx, name)

        ps = ctx.enter_context(nc.psum_tensor("ps", [P, 8, 512], F32))
        x = sb(ctx, "x", [P, B * NT, D])
        ident = sb(ctx, "ident", [P, P])
        ident_bf = sb(ctx, "ident_bf", [P, P], BF16)
        ln_stats = sb(ctx, "ln_stats", [P, NT, 6])
        ln_mv = sb(ctx, "ln_mv", [P, NT, 2])
        ln_var = sb(ctx, "ln_var", [P, NT])
        ln_sd = sb(ctx, "ln_sd", [P, NT])
        ln_r0 = sb(ctx, "ln_r0", [P, NT])
        ln_t = sb(ctx, "ln_t", [P, NT])
        ln_rs = sb(ctx, "ln_rs", [P, NT])
        x_stats = sb(ctx, "x_stats", [P, B * NT, 6])
        x_mv = sb(ctx, "x_mv", [P, B * NT, 2])
        x_var, x_sd, x_r0, x_t, x_rs = (sb(ctx, "x_" + part, [P, B * NT]) for part in ("var", "sd", "r0", "t", "rs"))

        def x_statistics(tile, ready):
            dve.after(ready)
            s = dve.did(nc.vector.bn_stats(x_stats[:, tile, :], x[:, tile, :]))
            dve.after(s)
            return dve.did(nc.vector.bn_aggr(x_mv[:, tile, :], x_stats[:, tile, :]))

        def rsqrt(var, sd, r0, t, rs, ready):
            act.after(ready)
            s = act.did(nc.scalar.activation(sd, var, ACT.Sqrt))
            yield
            dve.after(s)
            s = dve.did(nc.vector.reciprocal(r0, sd))
            dve.after(s)
            s = dve.did(nc.vector.tensor_tensor(t, r0, r0, ALU.mult))
            dve.after(s)
            s = dve.did(nc.vector.scalar_tensor_tensor(t, t, -0.5, var, ALU.mult, ALU.mult))
            dve.after(s)
            dve.did(nc.vector.scalar_tensor_tensor(rs, t, 1.5, r0, ALU.add, ALU.mult))

        def x_rsqrt():
            dve.after(dve.last)
            s = dve.did(nc.vector.tensor_scalar(x_var[:, :], x_mv[:, :, 1], LN_EPS, None, ALU.add))
            for _ in rsqrt(x_var[:, :], x_sd[:, :], x_r0[:, :], x_t[:, :], x_rs[:, :], s):
                pass
            return dve.last

        def x_normed(b, t, z, ready, free):
            i = NT * b + t
            dve.after(ready, free)
            return dve.did(nc.vector.tensor_scalar(z[:, t, :], x[:, i, :], x_mv[:, i, 0:1], x_rs[:, i:i + 1],
                                                   ALU.subtract, ALU.mult))

        def layer_norm(src, dst, ready, free):
            dve.after(ready)
            for t in range(NT):
                s = dve.did(nc.vector.bn_stats(ln_stats[:, t, :], src(t)))
                if t % 2:
                    yield
            dve.after(s)
            for t in range(NT):
                s = dve.did(nc.vector.bn_aggr(ln_mv[:, t, :], ln_stats[:, t, :]))
            dve.after(s)
            s = dve.did(nc.vector.tensor_scalar(ln_var[:, :], ln_mv[:, :, 1], LN_EPS, None, ALU.add))
            yield from rsqrt(ln_var[:, :], ln_sd[:, :], ln_r0[:, :], ln_t[:, :], ln_rs[:, :], s)
            dve.after(dve.last, free)
            for t in range(NT):
                s = dve.did(nc.vector.tensor_scalar(dst(t), src(t), ln_mv[:, t, 0:1], ln_rs[:, t:t + 1],
                                                    ALU.subtract, ALU.mult))
                if t % 2:
                    yield
            return s

        for lane in lanes:
            lane.phase("pair")

        x_in = [transfers(f"x_in{b}") for b in range(B)]
        x_dram = d["x"].rearrange("b (t p) n -> b p t n", p=P)
        x_in[0].start(sp, x[:, 0:NT, :], x_dram[0])
        s = pool.did(nc.gpsimd.memset(ident[:, :], 0.0))
        pool.after(s)
        s = pool.did(nc.gpsimd.affine_select(out=ident[:, :], in_=ident[:, :], compare_op=ALU.not_equal, fill=1.0,
                                             base=0, pattern=[[-1, P]], channel_multiplier=1))
        pool.after(s)
        ident_ready = pool.did(nc.gpsimd.tensor_copy(ident_bf[:, :], ident[:, :]))

        attn_a = ctx.enter_context(ExitStack())
        v_a = sb(attn_a, "v_a", [P, B, NT, HA, 2])
        qs = sb(attn_a, "qs", [STACK, B, 2, S], F32R)
        ks = sb(attn_a, "ks", [STACK, B, 2, S])
        mask = sb(attn_a, "mask", [P, B * NT, S], BF16)
        own_head = sb(attn_a, "own_head", [STACK, 16])
        wout_t = sb(attn_a, "wout_t", [KA + 1, D])
        sim = sb(attn_a, "sim", [P, 2, S + PAD])
        best = sb(attn_a, "best", [P, 8])
        small_a = transfers("small_a")

        core = Core()
        core.nc, core.d, core.ps, core.x, core.ident, core.ident_bf = nc, d, ps, x, ident, ident_bf
        core.pe, core.dve, core.act, core.pool, core.sp = lanes
        core.sb, core.phase, core.transfers = sb, phase, transfers
        core.x_statistics, core.x_rsqrt, core.x_normed = x_statistics, x_rsqrt, x_normed
        core.v_a, core.qs, core.ks, core.mask = v_a, qs, ks, mask
        core.own_head, core.wout_t, core.small_a = own_head, wout_t, small_a
        core.attn_a, core.side_banks, core.mask_done = attn_a, (4, 5), [None] * B
        lead, attention_a_rest = attention_a(core)

        pair = ctx.enter_context(ExitStack())
        h_neg = sb(pair, "h_neg", [F1, B * S])
        h_b1 = sb(pair, "h_b1", [F1, B * S])
        w2_t = sb(pair, "w2_t", [F1, F2])
        b2_twice = sb(pair, "b2_twice", [P, 1])
        w3_slide = sb(pair, "w3_slide", [P, 62])
        b3_all = sb(pair, "b3_all", [P, 1])
        small_pair = transfers("small_pair")
        y = sb(pair, "y", [P, NT, D])
        z = sb(pair, "z", [P, NT, D])
        xn_t = sb(pair, "xn_t", [P, ND, S])
        gamma = sb(pair, "gamma", [P, ND])
        beta = sb(pair, "beta", [P, ND])
        w1_t = sb(pair, "w1_t", [P, ND, F1])
        b1 = sb(pair, "b1", [F1, 1])
        wqkv_t = sb(pair, "wqkv_t", [P, ND, 3 * KA])
        b_qk = sb(pair, "b_qk", [P, 1])
        b_v = sb(pair, "b_v", [P, KA])
        qk = sb(pair, "qk", [P, S])
        qk_hi = sb(pair, "qk_hi", [P, S], F32R)
        qk_lo = sb(pair, "qk_lo", [P, S], F32R)
        weights = transfers("weights_a")
        for out, name in ((gamma, "gamma"), (beta, "beta"), (w1_t, "w1_t"), (b1, "b1"), (wqkv_t, "wqkv_t"),
                          (b_qk, "b_qk")):
            weights.start(sp, out[:], d[name])
        weights.start(sp, b_v[:, :], d["b_v"].partition_broadcast(P))
        small_pair.start(sp, w2_t[:, :], d["w2_t"])
        for half in range(2):
            small_pair.start(sp, b2_twice[F2 * half:F2 * half + F2, :], d["b2"])
        small_pair.start(sp, b3_all[:, :], d["b3"].partition_broadcast(P))
        s = pool.did(nc.gpsimd.memset(w3_slide[:, :], 0.0))
        sp.after(s)
        for half in range(2):
            small_pair.start(sp, w3_slide[F2 * half:F2 * half + F2, 30 + half:31 + half], d["w3_t"])
        for b in range(1, B):
            x_in[b].start(sp, x[:, NT * b:NT * b + NT, :], x_dram[b])
        small_a.start(sp, own_head[:, :], d["own_head"])
        small_a.start(sp, wout_t[0:KA, :], d["wout_t"])
        small_a.start(sp, wout_t[KA:KA + 1, :], d["bout"])
        pool.after(pool.last)
        q_zero = pool.did(nc.gpsimd.memset(qs[96:STACK, :, :, :].bitcast(F32), 0.0))
        pool.after(q_zero)
        k_one = pool.did(nc.gpsimd.memset(ks[96:STACK, :, :, :], 1.0))

        SIDE_BANKS = core.side_banks
        side_read = {bank: None for bank in SIDE_BANKS}
        n_side = [0]
        y_read, z_read, xn_read, qk_sent = [None], [None], [None], [None]
        stack_dmas = [transfers("stacks_even"), transfers("stacks_odd")]

        def side_bank():
            bank = SIDE_BANKS[n_side[0] % 2]
            n_side[0] += 1
            pe.after(side_read[bank])
            return bank

        def project(b):
            y_ready = yield from layer_norm(lambda t: x[:, NT * b + t, :], lambda t: y[:, t, :], x_in[b].all(),
                                            y_read[0])
            z_ready = yield from layer_norm(lambda t: y[:, t, :], lambda t: z[:, t, :], y_ready, z_read[0])
            pool.after(z_ready, k_one)
            for t in range(NT):
                y_read[0] = pool.did(nc.gpsimd.tensor_tensor(x[:, NT * b + t, :], x[:, NT * b + t, :], y[:, t, :],
                                                             ALU.add))
            pe.after(z_ready, ident_ready)
            act.after(weights.all(), xn_read[0])
            for k in range(ND):
                bank = side_bank()
                for t in range(NT):
                    s = nc.tensor.transpose(ps[:, bank, t * P:t * P + P], z[:, t, k * P:k * P + P], ident[:, :])
                s = z_read[0] = pe.did(s)
                act.after(s)
                xn_ready = side_read[bank] = act.did(nc.scalar.activation(
                    xn_t[:, k, :], ps[:, bank, :], ACT.Identity, bias=beta[:, k:k + 1], scale=gamma[:, k:k + 1]))
                yield
            pe.after(xn_ready, weights.all())
            bank = side_bank()
            for k in range(ND):
                s = nc.tensor.matmul(ps[:, bank, :], w1_t[:, ND - 1 - k, :], xn_t[:, ND - 1 - k, :], start=k == 0,
                                     stop=k == ND - 1)
            s = pe.did(s)
            act.after(s)
            s = act.did(nc.scalar.activation(h_neg[:, b * S:b * S + S], ps[:, bank, :], ACT.Copy, scale=-1.0))
            dve.after(s, weights.all())
            side_read[bank] = h_ready[b] = dve.did(nc.vector.tensor_scalar(h_b1[:, b * S:b * S + S], ps[:, bank, :],
                                                                           b1[:, 0:1], None, ALU.add))
            yield
            bank = side_bank()
            for k in range(ND):
                s = nc.tensor.matmul(ps[:, bank, :], wqkv_t[:, k, 0:2 * KA], xn_t[:, k, :], start=k == 0,
                                     stop=k == ND - 1)
            s = pe.did(s)
            act.after(s)
            s = side_read[bank] = act.did(nc.scalar.activation(qk[:, :], ps[:, bank, :], ACT.Identity,
                                                               bias=b_qk[:, 0:1]))
            yield
            dve.after(s, qk_sent[0])
            s = dve.did(nc.vector.tensor_copy(qk_hi[:, :], qk[:, :]))
            dve.after(s)
            qk_split = dve.did(nc.vector.tensor_tensor(qk_lo[:, :], qk[:, :], qk_hi[:, :].bitcast(F32),
                                                       ALU.subtract))
            sp.after(qk_split)
            for u in range(2):
                for t, (q_src, k_src) in enumerate(((qk_hi, qk_hi), (qk_lo, qk_hi), (qk_hi, qk_lo))):
                    for dst, src, first in ((qs, q_src, 0), (ks, k_src, KA)):
                        at = first + 32 * u
                        qk_sent[0] = stack_dmas[b % 2].start(sp, dst[32 * t:32 * t + 32, b, u, :].bitcast(F32),
                                                             src[at:at + 32, :].bitcast(F32))
            yield
            bank = side_bank()
            for t in range(NT):
                for k in range(ND):
                    s = nc.tensor.matmul(ps[:, bank, t * KA:t * KA + KA], xn_t[:, k, t * P:t * P + P],
                                         wqkv_t[:, k, 2 * KA:3 * KA], start=k == 0, stop=k == ND - 1)
            s = xn_read[0] = pe.did(s)
            dve.after(s)
            for t in range(NT):
                side_read[bank] = dve.did(nc.vector.tensor_tensor(
                    v_a[:, b, t, :, :].rearrange("p h e -> p (h e)"), ps[:, bank, t * KA:t * KA + KA], b_v[:, :],
                    ALU.add))
            yield

        h_ready = [None] * B
        for _ in project(0):
            pass

        with ExitStack() as mem:
            N_PAIR = 16
            pair_in = sb(mem, "pair_in", [F1, N_PAIR, S])
            NG = 4
            pair_mid = sb(mem, "pair_mid", [P, NG, 2, S])
            in_read = [None] * N_PAIR
            mid_read = [None] * NG
            group_read = [None] * 2
            sim_bank_read = [None] * 2
            sim_free = [None] * 2
            for lane in (pe, act, dve):
                lane.after(small_pair.all())

            def row_of(tile, r, c, half):
                return tile * P + 32 * c + 2 * r + half

            def top_k(tile, sim_ready):
                w = tile % 2
                row = sim[:, w, :]

                def round_(n):
                    def go():
                        dve.after(sim_ready if n == 0 else dve.last)
                        s = dve.did(nc.vector.max(best[:, :], row))
                        dve.after(s)
                        dve.did(nc.vector.match_replace(row, best[:, :], row, TAKEN))
                    return go

                def keep():
                    dve.after(dve.last)
                    sim_free[w] = core.mask_done[tile // NT] = dve.did(nc.vector.tensor_scalar(
                        mask[:, tile, :], sim[:, w, 0:S], KEPT_ABOVE, MASKED, ALU.is_gt, ALU.mult))
                return [round_(n) for n in range((TOPK + PAD) // 8)] + [keep]

            rounds = []

            def finish_tile(tile, sims_done):
                w = tile % 2
                act.after(sims_done, sim_free[w])
                s = sim_bank_read[w] = act.did(nc.scalar.activation(sim[:, w, 0:S], ps[:, 6 + w, :], ACT.Identity,
                                                                    bias=b3_all[:, 0:1]))
                pool.after(sim_free[w])
                pool.did(nc.gpsimd.memset(sim[:, w, S:S + PAD], SENTINEL))
                pool.after(s)
                s = pool.did(nc.gpsimd.affine_select(out=sim[:, w, 0:S], in_=sim[:, w, 0:S],
                                                     compare_op=ALU.not_equal, fill=0.0, base=(tile % NT) * P,
                                                     pattern=[[-1, S]], channel_multiplier=1))
                return top_k(tile, s)

            def second_layer(step):
                tile, r, groups = step
                w = tile % 2
                if r == 0:
                    pe.after(sim_bank_read[w])
                for g, (slot, ready) in enumerate(groups):
                    pe.after(ready)
                    for k in range(2):
                        c = 2 * g + k
                        s = nc.tensor.matmul(ps[32 * c:32 * c + 32, 6 + w, :], w3_slide[:, 30 - 2 * r:62 - 2 * r],
                                             pair_mid[:, slot, k, :], start=r == 0, stop=r == 15)
                    mid_read[slot] = s = pe.did(s)
                return s

            behind = None
            n_in = n_group = 0
            projecting = iter(())
            for tile in range(B * NT):
                b = tile // NT
                if tile % NT == 0:
                    for _ in projecting:
                        pass
                    dve.after(h_ready[b])
                    projecting = project(b + 1) if b + 1 < B else iter(())
                for r in range(16):
                    groups = []
                    for g in range(2):
                        slots = []
                        for k in range(2):
                            for half in range(2):
                                i = row_of(tile, r, 2 * g + k, half)
                                slot = n_in % N_PAIR
                                n_in += 1
                                dve.after(in_read[slot])
                                first_ready = dve.did(nc.vector.tensor_scalar(
                                    pair_in[:, slot, :], h_neg[:, b * S:b * S + S], h_b1[:, i:i + 1], 0.0,
                                    ALU.add, ALU.max))
                                slots.append((slot, k, half))
                        bank = 2 * (n_group % 2)
                        pe.after(group_read[n_group % 2], first_ready)
                        for slot, k, half in slots:
                            s = nc.tensor.matmul(ps[F2 * half:F2 * half + F2, bank + k, :], w2_t[:, :],
                                                 pair_in[:, slot, :], start=True, stop=True)
                        s = pe.did(s)
                        for slot, _, _ in slots:
                            in_read[slot] = s
                        mid = n_group % NG
                        act.after(s, mid_read[mid])
                        ready = group_read[n_group % 2] = act.did(nc.scalar.activation(
                            pair_mid[:, mid, :, :], ps[:, bank:bank + 2, :], ACT.Relu, bias=b2_twice[:, 0:1]))
                        groups.append((mid, ready))
                        n_group += 1
                    if behind:
                        s = second_layer(behind)
                        if behind[1] == 15:
                            rounds += finish_tile(behind[0], s)
                    behind = (tile, r, groups)
                    if r % 2 and rounds:
                        rounds.pop(0)()
                    if r % 2 == 0:
                        next(projecting, None)
                    if tile >= B * NT - 5:
                        if tile == B * NT - 5 and r == 0:
                            pe.after(*side_read.values(), *(dmas.all() for dmas in stack_dmas), k_one)
                            for lane in (dve, act):
                                lane.after(small_a.all(), *(dmas.all() for dmas in stack_dmas), k_one)
                        next(lead, None)
            s = second_layer(behind)
            rounds += finish_tile(behind[0], s)
            core.last_rounds = rounds

        for lane in lanes:
            lane.after(*(dmas.all() for dmas in stack_dmas))
        pair.close()

        for _ in lead:
            pass
        attention_a_rest()
        attn_a.close()

        out_dram = d["out"].rearrange("b (t p) n -> b p t n", p=P)
        stored = transfers("stored")

        def store(tile, ready):
            sp.after(ready)
            if tile % NT == NT - 1:
                stored.start(sp, out_dram[tile // NT], x[:, tile + 1 - NT:tile + 1, :])

        feed_forward(core, "ffn1", x_statistics)
        attention_b(core)
        feed_forward(core, "ffn2", store)
        sp.after(stored.all())


def attention_a(k):
    nc, pe, dve, act, pool, sp, ps, x = k.nc, k.pe, k.dve, k.act, k.pool, k.sp, k.ps, k.x
    LEAD, CHUNK, N_KM, N_EX = 18, 16, 3, (6, 7)
    HEADS = B * HA
    km = k.sb(k.attn_a, "km", [STACK, 2 * N_KM, S], F32R)
    maxes = k.sb(k.attn_a, "maxes", [P, 2, NT, CHUNK])
    unused = k.sb(k.attn_a, "unused", [P, 2, S], BF16)

    n_km = [0, 0]
    km_read = [None] * (2 * N_KM)
    o1_read, o2_read = [None] * 2, [None] * 2
    max_read, max_sent = [None] * 2, [None] * 2
    maxes_ready = {}
    counts = {"o1": 0, "group": 0}
    o1_banks = k.side_banks

    def one_head(engine, kind, n):
        b, u, a = n // HA, n // CHUNK % 2, n % CHUNK
        slot = kind * N_KM + n_km[kind] % N_KM
        n_km[kind] += 1
        engine.after(km_read[slot])
        own = k.own_head[:, a:a + 1]
        if engine is act:
            return slot, act.did(nc.scalar.activation(km[:, slot, :], k.ks[:, b, u, :], ACT.Copy, scale=own))
        return slot, dve.did(nc.vector.tensor_scalar(km[:, slot, :], k.ks[:, b, u, :], own, None, ALU.mult))

    def stack_of(engine, kind, n):
        made = ahead[kind].pop(n, None) or one_head(engine, kind, n)
        if n + 1 < HEADS:
            ahead[kind][n + 1] = one_head(engine, kind, n + 1)
        return made

    ahead = ({}, {})

    def scores(n, t):
        b, u, a, w = n // HA, n // CHUNK % 2, n % CHUNK, n // CHUNK % 2
        if t == 0:
            own_stack[0] = stack_of(dve, 0, n)
        slot, ready = own_stack[0]
        which = counts["o1"] % 2
        bank = o1_banks[which]
        counts["o1"] += 1
        pe.after(ready, o1_read[which])
        s = km_read[slot] = pe.did(nc.tensor.matmul(ps[:, bank, :], k.qs[:, b, u, t * P:t * P + P], km[:, slot, :],
                                                    start=True, stop=True))

        def reduce():
            dve.after(s, o1_read[which], k.mask_done[b], max_read[w] if a == 0 else None)
            o1_read[which] = maxes_ready[n // CHUNK] = dve.did(nc.vector.tensor_tensor_reduce(
                unused[:, which, :], ps[:, bank, :], k.mask[:, NT * b + t, :], 1.0, TAKEN, ALU.add, ALU.max,
                maxes[:, w, t, a:a + 1]))
        return reduce

    own_stack = [None]

    def maxima(n):
        for t in range(NT):
            scores(n, t)()
            yield

    def lead():
        waiting = []
        for n in range(LEAD):
            for t in range(NT):
                if len(waiting) == len(o1_banks):
                    waiting.pop(0)()
                waiting.append(scores(n, t))
                yield
        for reduce in waiting:
            reduce()

    def rest():
        k.phase("attn_a")
        nonlocal o1_banks
        o1_banks = (0, 1)
        with ExitStack() as mem:
            mask_t = k.sb(mem, "mask_t", [P, 2, NT, S], BF16)
            v_aug = k.sb(mem, "v_aug", [P, 2, NT, HA, 3])
            ex = k.sb(mem, "ex", [P, sum(N_EX), 2, S])
            max_t = k.sb(mem, "max_t", [CHUNK, 2, S], F32R)
            ao_t = k.sb(mem, "ao_t", [P, 2, HA // 4, S])
            ao = k.sb(mem, "ao", [P, 2, HA, 2])
            r_den = k.sb(mem, "r_den", [P, HA])
            ao_feat = k.sb(mem, "ao_feat", [KA + 1, 2, P])

            OUT_BANK, SIDE_BANK = 6, 7
            pool.after(k.small_a.all())
            s = pool.did(nc.gpsimd.memset(v_aug[:, :, :, :, 2:3], 1.0))
            pool.after(s)
            one_row = pool.did(nc.gpsimd.memset(ao_feat[KA:KA + 1, :, :], 1.0))
            pool.after(one_row)
            bank_zero = dve.did(nc.vector.memset(ps[:, OUT_BANK, :], 0.0))
            pe.after(k.small_a.all(), bank_zero, one_row)
            for lane in (dve, act):
                lane.after(k.small_a.all())

            max_dmas = [k.transfers("maxima_even"), k.transfers("maxima_odd")]
            in_place = {}
            mask_ready = [None] * B
            mask_read = [None] * B
            v_ready, v_read = [None] * B, [None] * B
            ex_read = [None] * sum(N_EX)
            ao_read = [None] * 2
            side_read = [None]

            def place_maxima(chunk):
                b, u, w = chunk // 2, chunk % 2, chunk % 2
                pe.after(maxes_ready[chunk], side_read[0])
                for t in range(NT):
                    s = nc.tensor.transpose(ps[0:CHUNK, SIDE_BANK, t * P:t * P + P], maxes[:, w, t, :], k.ident[:, :])
                s = max_read[w] = pe.did(s)
                act.after(s, max_sent[w])
                s = side_read[0] = act.did(nc.scalar.activation(max_t[:, w, :], ps[0:CHUNK, SIDE_BANK, :], ACT.Copy,
                                                                scale=-1.0))
                sp.after(s, km_read[(n_km[0] - 1) % N_KM])
                in_place[chunk] = max_sent[w] = max_dmas[w].start(sp, k.qs[96:STACK, b, u, :].bitcast(F32),
                                                                  max_t[:, w, :].bitcast(F32))

            def turn_mask(b, t):
                w = b % 2
                bank = ps[:, SIDE_BANK, 0:S // 2].bitcast(BF16)
                pe.after(side_read[0])
                for i in range(NT):
                    s = nc.tensor.transpose(bank[:, i * P:i * P + P], k.mask[:, NT * b + i, t * P:t * P + P],
                                            k.ident_bf[:, :])
                s = pe.did(s)
                act.after(s, mask_read[b - 2] if b >= 2 else None)
                mask_ready[b] = side_read[0] = act.did(nc.scalar.activation(mask_t[:, w, t, :], bank, ACT.Copy))

            def values(b):
                w = b % 2
                pool.after(v_read[b - 2] if b >= 2 else None)
                v_ready[b] = pool.did(nc.gpsimd.tensor_copy(
                    v_aug[:, w, :, :, 0:2].rearrange("p t h e -> p (t h) e"),
                    k.v_a[:, b, :, :, :].rearrange("p t h e -> p (t h) e")))

            def exponentials(n, out):
                b, u, w = n // HA, n // CHUNK % 2, (n // HA) % 2
                slot, ready = stack_of(act, 1, n)
                pe.after(ready, in_place[n // CHUNK], mask_ready[b])
                for g in range(NT // 2):
                    pair_of_banks, e = counts["group"] % 2, g * N_EX[0] + n % N_EX[g]
                    counts["group"] += 1
                    bank = 2 + 2 * pair_of_banks
                    pe.after(o2_read[pair_of_banks])
                    for j in range(2):
                        t = 2 * g + j
                        nc.tensor.matmul(ps[:, bank + j, :], k.ident_bf[:, :], mask_t[:, w, t, :], start=True, stop=False)
                        s = nc.tensor.matmul(ps[:, bank + j, :], km[:, slot, t * P:t * P + P], k.qs[:, b, u, :],
                                             start=False, stop=True)
                    s = pe.did(s)
                    act.after(s, ex_read[e])
                    s2 = o2_read[pair_of_banks] = act.did(nc.scalar.activation(
                        ex[:, e, :, :], ps[:, bank:bank + 2, :], ACT.Exp, scale=2.0 ** -0.5))
                    out.append((e, s2))
                    km_read[slot] = s
                    mask_read[b] = s
                    yield

            def weighted(n, groups):
                b, w, block = n // HA, (n // HA) % 2, n % HA // 4
                pe.after(v_ready[b], out_read[0])
                for t in range(NT):
                    for g in range(4):
                        e, ready = groups[g][t // 2]
                        pe.after(ready)
                        s = nc.tensor.matmul(ps[32 * g:32 * g + 3, OUT_BANK, :], v_aug[:, w, t, 4 * block + g, :],
                                             ex[:, e, t % 2, :], start=t == 0, stop=t == NT - 1)
                    s = pe.did(s)
                    for g in groups:
                        ex_read[g[t // 2][0]] = s
                    if t < NT - 1:
                        yield
                v_read[b] = s
                act.after(s, ao_read[w] if block == 0 else None)
                s = out_read[0] = act.did(nc.scalar.activation(ao_t[:, w, block, :], ps[:, OUT_BANK, :], ACT.Copy))
                if block == HA // 4 - 1:
                    side[:0] = finish(b, s)
                yield

            out_read = [bank_zero]

            def finish(b, ao_ready):
                w = b % 2
                banks = (SIDE_BANK,) if b < B - 1 else (SIDE_BANK,) + o1_banks
                bank_read = dict(zip(o1_banks, o1_read))
                count, ao_done, feat_done = [0], {}, {}

                def next_bank():
                    bank = banks[count[0] % len(banks)]
                    count[0] += 1
                    pe.after(side_read[0] if bank == SIDE_BANK else bank_read[bank])
                    return bank

                def read(bank, signal):
                    if bank == SIDE_BANK:
                        side_read[0] = signal
                    bank_read[bank] = signal

                def divide(t, half):
                    pe.after(ao_ready)
                    bank = next_bank()
                    for i in range(4):
                        s = nc.tensor.transpose(ps[:, bank, i * P:i * P + P],
                                                ao_t[:, w, 4 * half + i, t * P:t * P + P], k.ident[:, :])
                    s = pe.did(s)
                    ao_read[w] = s
                    sums = ps[:, bank, :].rearrange("p (h r) -> p h r", r=32)
                    part = r_den[:, 16 * half:16 * half + 16]
                    dve.after(s)
                    s = dve.did(nc.vector.reciprocal(part, sums[:, :, 2]))
                    dve.after(s)
                    for e in range(2):
                        s = dve.did(nc.vector.tensor_tensor(ao[:, t % 2, 16 * half:16 * half + 16, e], sums[:, :, e],
                                                            part, ALU.mult))
                    ao_done[t] = s
                    read(bank, s)

                def turn(t):
                    pe.after(ao_done[t])
                    bank = next_bank()
                    s = pe.did(nc.tensor.transpose(ps[0:KA, bank, 0:P],
                                                   ao[:, t % 2, :, :].rearrange("p h e -> p (h e)"), k.ident[:, :]))
                    act.after(s)
                    feat_done[t] = act.did(nc.scalar.activation(ao_feat[0:KA, t % 2, :], ps[0:KA, bank, 0:P],
                                                                ACT.Copy))
                    read(bank, feat_done[t])

                def project(t):
                    pe.after(feat_done[t])
                    bank = next_bank()
                    s = pe.did(nc.tensor.matmul(ps[:, bank, :], ao_feat[:, t % 2, :], k.wout_t[:, :], start=True,
                                                stop=True))
                    dve.after(s)
                    s = dve.did(nc.vector.tensor_tensor(x[:, NT * b + t, :], x[:, NT * b + t, :], ps[:, bank, :],
                                                        ALU.add))
                    read(bank, s)
                    k.x_statistics(NT * b + t, s)

                steps = []
                for t in range(NT + 2):
                    if t < NT:
                        steps += [lambda t=t, half=half: divide(t, half) for half in range(2)]
                    if 1 <= t <= NT:
                        steps.append(lambda t=t - 1: turn(t))
                    if t >= 2:
                        steps.append(lambda t=t - 2: project(t))
                return steps

            side = []
            values(0)
            for t in range(NT):
                turn_mask(0, t)
            place_maxima(0)
            groups = []
            behind = iter(())
            for n in range(HEADS + 4):
                b, h = n // HA, n % HA
                if h == 4 and b + 1 < B:
                    values(b + 1)
                    side += [lambda t=t, b=b: turn_mask(b + 1, t) for t in range(NT)]
                if k.last_rounds:
                    k.last_rounds.pop(0)()
                groups.append([])
                ahead_steps = maxima(n + LEAD) if n + LEAD < HEADS else iter(())
                own_steps = exponentials(n, groups[-1]) if n < HEADS else iter(())
                for steps in (own_steps, ahead_steps, behind, ahead_steps, own_steps, ahead_steps):
                    next(steps, None)
                if side:
                    side.pop(0)()
                for _ in ahead_steps:
                    pass
                next(own_steps, None)
                if (n + LEAD) % CHUNK == 0 and n + LEAD <= HEADS:
                    place_maxima((n + LEAD) // CHUNK - 1)
                if h % 4 == 3:
                    behind, groups = weighted(n - 3, groups), []
            for step in side:
                step()

    return lead(), rest


def feed_forward(k, name, tile_done):
    nc, pe, dve, act, pool, sp, ps, x = k.nc, k.pe, k.dve, k.act, k.pool, k.sp, k.ps, k.x
    k.phase(name)
    OC = 2
    CHUNKS = NI // OC
    WU, WD = ND * 2 * OC * P, OC * D
    with ExitStack() as mem:
        raw = k.sb(mem, name + "_raw", [P, 2, WU + WD])
        w_hi = k.sb(mem, name + "_w_hi", [P, 2, WU + WD], F32R)
        w_lo = k.sb(mem, name + "_w_lo", [P, 2, WU + WD], F32R)
        z = k.sb(mem, name + "_z", [P, NT, D])
        z_hi = k.sb(mem, name + "_z_hi", [P, ND, B * S], F32R)
        z_lo = k.sb(mem, name + "_z_lo", [P, ND, B * S], F32R)
        silu = k.sb(mem, name + "_silu", [P, 2, S])
        inner = k.sb(mem, name + "_inner", [P, 2, S])
        in_hi = k.sb(mem, name + "_in_hi", [P, 2, OC, S], F32R)
        in_lo = k.sb(mem, name + "_in_lo", [P, 2, OC, S], F32R)
        loads = [k.transfers(f"{name}_w{i}") for i in range(2)]
        w_read = [None] * 2
        raw_read = [[], []]
        w_ready = {}
        z_ready, z_free = {}, None
        bank_read = [None] * 8
        silu_read, in_read = [None] * 2, [None] * 2

        def load(c):
            w = c % 2
            sp.after(*raw_read[w])
            return loads[w].start(sp, raw[:, w, :], k.d["w_ffn"][c])

        def split(c, arrived):
            w = c % 2
            act.after(arrived, w_read[w])
            w_ready[c] = []
            for a, e in ((0, WU // 2), (WU // 2, WU), (WU, WU + WD)):
                s = act.did(nc.scalar.activation(w_hi[:, w, a:e], raw[:, w, a:e], ACT.Copy))
                pool.after(s)
                s = pool.did(nc.gpsimd.tensor_tensor(w_lo[:, w, a:e], raw[:, w, a:e], w_hi[:, w, a:e].bitcast(F32),
                                                     ALU.subtract))
                w_ready[c].append(s)
            raw_read[w] = [s]

        def normed(b):
            for t in range(NT):
                s = k.x_normed(b, t, z, rs_ready, z_read[0])
            yield
            pe.after(s)
            for f in range(ND):
                bank = 6 + f % 2
                pe.after(bank_read[bank])
                for t in range(NT):
                    s = nc.tensor.transpose(ps[:, bank, t * P:t * P + P], z[:, t, f * P:f * P + P], k.ident[:, :])
                s = z_read[0] = pe.did(s)
                act.after(s)
                at = slice(b * S, b * S + S)
                s = act.did(nc.scalar.activation(z_hi[:, f, at], ps[:, bank, :], ACT.Copy))
                dve.after(s)
                bank_read[bank] = z_ready[b] = dve.did(nc.vector.tensor_tensor(
                    z_lo[:, f, at], ps[:, bank, :], z_hi[:, f, at].bitcast(F32), ALU.subtract))
                if f % 2:
                    yield

        def up(c, b, o):
            w = c % 2
            for g in range(2):
                bank = 2 * (o % 2) + g
                pe.after(bank_read[bank])
                n = 0
                for z_part, w_part in ((z_hi, w_hi), (z_lo, w_hi), (z_hi, w_lo)):
                    for f in range(ND):
                        at = (f * 2 + g) * OC * P + o * P
                        s = nc.tensor.matmul(ps[:, bank, :], w_part[:, w, at:at + P], z_part[:, f, b * S:b * S + S],
                                             start=n == 0, stop=n == 3 * ND - 1)
                        n += 1
                s = pe.did(s)
                if g == 0:
                    act.after(s, silu_read[o % 2])
                    gate = bank_read[bank] = act.did(nc.scalar.activation(silu[:, o % 2, :], ps[:, bank, :], ACT.Silu))
            u = (c * B + b) % 2
            dve.after(s, gate)
            s = silu_read[o % 2] = bank_read[bank] = dve.did(nc.vector.tensor_tensor(
                inner[:, o % 2, :], silu[:, o % 2, :], ps[:, bank, :], ALU.mult))
            dve.after(s, in_read[u])
            s = dve.did(nc.vector.tensor_copy(in_hi[:, u, o, :], inner[:, o % 2, :]))
            dve.after(s)
            return dve.did(nc.vector.tensor_tensor(in_lo[:, u, o, :], inner[:, o % 2, :], in_hi[:, u, o, :].bitcast(F32),
                                                   ALU.subtract))

        def down(c, b, t, ready):
            w, u = c % 2, (c * B + b) % 2
            bank = 4 + t % 2
            pe.after(ready, w_ready[c][2], bank_read[bank])
            n = 0
            for i_part, w_part in ((in_hi, w_hi), (in_lo, w_hi), (in_hi, w_lo)):
                for o in range(OC):
                    s = nc.tensor.matmul(ps[:, bank, :], i_part[:, u, o, t * P:t * P + P],
                                         w_part[:, w, WU + o * D:WU + o * D + D], start=n == 0, stop=n == 3 * OC - 1)
                    n += 1
            s = pe.did(s)
            in_read[u] = s
            if b == B - 1:
                w_read[w] = s
            dve.after(s, x_done[b])
            bank_read[bank] = dve.did(nc.vector.tensor_tensor(x[:, NT * b + t, :], x[:, NT * b + t, :], ps[:, bank, :],
                                                              ALU.add))
            if c == CHUNKS - 1:
                tile_done(NT * b + t, bank_read[bank])
            return bank_read[bank]

        z_read = [None]
        x_done = [None] * B
        arrived = [load(0), load(1)]
        rs_ready = k.x_rsqrt()
        split(0, arrived[0])
        for _ in normed(0):
            pass
        behind = None
        for c in range(CHUNKS):
            for b in range(B):
                pe.after(w_ready[c][1], z_ready[b])
                norm = normed(b + 1) if c == 0 and b + 1 < B else iter(())
                next(norm, None)
                for o in range(OC):
                    s = up(c, b, o)
                    next(norm, None)
                    if behind:
                        for t in range(2 * o, 2 * o + 2):
                            s_x = down(*behind[:2], t, behind[2])
                        if o == OC - 1:
                            x_done[behind[1]] = s_x
                behind = (c, b, s)
                for _ in norm:
                    pass
                if b == 0 and c + 1 < CHUNKS:
                    split(c + 1, arrived[(c + 1) % 2])
                    if c + 2 < CHUNKS:
                        arrived[c % 2] = load(c + 2)
        for t in range(NT):
            down(*behind[:2], t, behind[2])


def attention_b(k):
    nc, pe, dve, act, pool, sp, ps, x, d = k.nc, k.pe, k.dve, k.act, k.pool, k.sp, k.ps, k.x, k.d
    k.phase("attn_b")
    ROWS, N_EX, HU, SCALE = 97, 10, 4, HDB ** -0.5
    UNITS = B * (HB // HU)
    with ExitStack() as mem:
        w_qk = k.sb(mem, "wb_qk", [P, ND, HB // HU, 2, P])
        w_v = k.sb(mem, "wb_v", [P, ND, D])
        w_proj = k.sb(mem, "wb_proj", [P, ND, D])
        z = k.sb(mem, "zb", [P, NT, D])
        z_t = k.sb(mem, "zb_t", [P, 2, ND, S])
        hi = k.sb(mem, "hi_b", [P, 2, S], F32R)
        lo = k.sb(mem, "lo_b", [P, 2, S], F32R)
        q_stack = k.sb(mem, "q_stack", [ROWS, 3, HU, S], F32R)
        k_stack = k.sb(mem, "k_stack", [ROWS, 3, HU, S], F32R)
        v = k.sb(mem, "vb", [P, 2, NT, D])
        ex = k.sb(mem, "ex_b", [P, N_EX, S])
        ex_sum = k.sb(mem, "ex_sum", [P, HU, S])
        out_t = k.sb(mem, "out_t", [P, ND, S])
        sums_sb = k.sb(mem, "sums_sb", [P, 2, S])
        maxes = k.sb(mem, "maxes_b", [P, 2, HU, NT])
        max_t = k.sb(mem, "max_t_b", [HU, 2, S], F32R)
        ones = k.sb(mem, "ones_b", [P, 32])
        lam_in = ex[0:1, 0:4, :]
        lam_unused = ex[0:1, 4:6, :]
        lam = k.sb(mem, "lam", [1, 4])
        q2_row = k.sb(mem, "q2_row", [1, P])
        q1_col = k.sb(mem, "q1_col", [P, 1])
        q_scale = k.sb(mem, "q_scale", [P, 1])

        halves = nc.dram_tensor("halves", (2, 2, P, 2, S), F32).ap()
        halves_dmas = [k.transfers("halves_even"), k.transfers("halves_odd")]

        O1_BANKS, O2_BANKS, SUM_BANK, SIDE_BANKS = (0, 1, 2), (3, 4), 5, (6, 7)
        rs_ready = k.x_rsqrt()
        small = k.transfers("small_b")
        small.start(sp, lam_in[:, :, :], d["lambdas"])
        small.start(sp, q2_row[:, :], d["q2_row"])
        small.start(sp, q1_col[:, :], d["q1_col"])
        qk_weights, v_weights, proj_weights = (k.transfers(f"weights_b_{part}") for part in ("qk", "v", "proj"))
        qk_weights.start(sp, w_qk[:, :, :, :, :], d["wb_qk"])
        v_weights.start(sp, w_v[:, :, :], d["wb_v"])

        s = pool.did(nc.gpsimd.memset(ones[:, :], 1.0))
        pool.after(s)
        s = pool.did(nc.gpsimd.memset(k_stack[96:97, :, :, :].bitcast(F32), 1.0))
        ones_ready = s

        side_read = {bank: None for bank in SIDE_BANKS}
        q_scale_ready = [None]
        n_side = [0]
        z_read, z_ready, z_t_read, z_t_ready = [None], [None], [None] * B, [None] * B
        o1_read, o2_read = [None] * len(O1_BANKS), [None] * len(O2_BANKS)
        ex_read, added = [None] * N_EX, [None] * N_EX
        v_ready, v_read = [None] * B, [None] * B
        sum_read, out_read, ex_sum_read, sums_free = [ones_ready], [None], [None], [None]
        product_done = [[None] * 2 for _ in range(UNITS)]
        stack_dmas = [k.transfers(f"stacks_b{i}") for i in range(3)]
        max_dmas = [k.transfers("maxima_b_even"), k.transfers("maxima_b_odd")]
        stacked, hi_sent = [None] * UNITS, [None]
        in_place = [None] * UNITS
        max_ready, o2_last = [None] * UNITS, [None] * UNITS
        max_read = [None] * 2
        ex_sum_ready = [None] * HU
        n_o2 = [0]

        def query_scale():
            dve.after(small.all())
            for i in range(2):
                s = dve.did(nc.vector.tensor_tensor_reduce(
                    lam_unused[:, i, :], lam_in[:, 2 * i, :], lam_in[:, 2 * i + 1, :], 1.0, 0.0, ALU.mult, ALU.add,
                    lam[:, i:i + 1]))
            act.after(s)
            s = act.did(nc.scalar.activation(lam[:, 2:4], lam[:, 0:2], ACT.Exp))
            dve.after(s)
            s = dve.did(nc.vector.tensor_tensor(lam[:, 0:1], lam[:, 3:4], lam[:, 2:3], ALU.subtract))
            dve.after(s)
            s = dve.did(nc.vector.tensor_scalar(lam[:, 1:2], lam[:, 0:1], -LAMBDA_INIT, None, ALU.add))
            pe.after(s, side_read[SIDE_BANKS[0]])
            s = pe.did(nc.tensor.matmul(ps[:, SIDE_BANKS[0], 0:1], q2_row[:, :], lam[:, 1:2], start=True, stop=True))
            dve.after(s)
            q_scale_ready[0] = side_read[SIDE_BANKS[0]] = dve.did(nc.vector.tensor_tensor(
                q_scale[:, :], ps[:, SIDE_BANKS[0], 0:1], q1_col[:, :], ALU.add))

        def side_bank():
            bank = SIDE_BANKS[n_side[0] % 2]
            n_side[0] += 1
            pe.after(side_read[bank])
            return bank

        def norm_steps(b):
            def norm(t):
                z_ready[0] = k.x_normed(b, t, z, rs_ready, z_read[0])
            light[:0] = [lambda t=t: norm(t) for t in range(NT)]
            steps = []
            for f in range(ND):
                def turn(f=f):
                    pe.after(z_ready[0])
                    bank = side_bank()
                    for t in range(NT):
                        s = nc.tensor.transpose(ps[:, bank, t * P:t * P + P], z[:, t, f * P:f * P + P], k.ident[:, :])
                    s = z_read[0] = pe.did(s)
                    act.after(s, z_t_read[b - 2] if b >= 2 else None)
                    side_read[bank] = z_t_ready[b] = act.did(nc.scalar.activation(z_t[:, b % 2, f, :], ps[:, bank, :],
                                                                                  ACT.Copy))
                steps.append(turn)
            for t in range(NT):
                def values(t=t):
                    pe.after(z_t_ready[b], v_weights.all())
                    bank = side_bank()
                    for f in range(ND):
                        s = nc.tensor.matmul(ps[:, bank, :], z_t[:, b % 2, f, t * P:t * P + P], w_v[:, f, :],
                                             start=f == 0, stop=f == ND - 1)
                        if f == ND // 2 - 1:
                            yield
                    s = pe.did(s)
                    act.after(s, v_read[b - 2] if b >= 2 else None)
                    side_read[bank] = v_ready[b] = act.did(nc.scalar.activation(v[:, b % 2, t, :], ps[:, bank, :],
                                                                                ACT.Copy))
                steps.append(values)
            return steps

        def query_key_steps(n):
            b, c, w = n // (HB // HU), n % (HB // HU), n % 3
            steps = []
            for i in range(2):
                def product(i=i):
                    pe.after(z_t_ready[b], qk_weights.all())
                    bank = side_bank()
                    for f in range(ND):
                        s = nc.tensor.matmul(ps[:, bank, :], w_qk[:, f, c, i, :], z_t[:, b % 2, f, :], start=f == 0,
                                             stop=f == ND - 1)
                        if f == ND // 2 - 1:
                            yield
                    s = pe.did(s)
                    z_t_read[b] = s
                    act.after(s, hi_sent[0], q_scale_ready[0])
                    scale = 1.0 if i else q_scale[:, 0:1]
                    s = act.did(nc.scalar.activation(hi[:, i, :], ps[:, bank, :], ACT.Copy, scale=scale))
                    dve.after(s)
                    side_read[bank] = product_done[n][i] = dve.did(nc.vector.scalar_tensor_tensor(
                        lo[:, i, :], ps[:, bank, :], scale, hi[:, i, :].bitcast(F32), ALU.mult, ALU.subtract))
                steps.append(product)

            def send():
                sp.after(*product_done[n], o2_last[n - 3] if n >= 3 else None, ones_ready)
                for half, part in enumerate((hi, lo)):
                    sent = halves_dmas[n % 2].start(sp, halves[n % 2, half], part[:, :, :].bitcast(F32))
                sp.after(sent)
                for r, (q_half, k_half) in enumerate(((0, 0), (1, 0), (0, 1))):
                    for stack, half, i in ((q_stack, q_half, 0), (k_stack, k_half, 1)):
                        stacked[n] = stack_dmas[w].start(sp, stack[32 * r:32 * r + 32, w, :, :].bitcast(F32),
                                                         halves[n % 2, half, :, i, :].rearrange("(g p) s -> p g s", g=HU))
                hi_sent[0] = sent
            return steps + [send]

        def maxima(n):
            w, s3 = n % 2, n % 3
            pe.after(stacked[n])
            dve.after(max_read[w])
            for i in range(HU * NT):
                g, t = i // NT, i % NT
                o = (n * HU * NT + i) % len(O1_BANKS)
                bank = O1_BANKS[o]
                pe.after(o1_read[o])
                s = pe.did(nc.tensor.matmul(ps[:, bank, :], q_stack[0:ROWS - 1, s3, g, t * P:t * P + P],
                                            k_stack[0:ROWS - 1, s3, g, :], start=True, stop=True))
                dve.after(s)
                o1_read[o] = max_ready[n] = dve.did(nc.vector.tensor_reduce(maxes[:, w, g, t:t + 1], ps[:, bank, :],
                                                                            AX.X, ALU.max))
                yield

        def place_maxima(n):
            w = n % 2
            pe.after(max_ready[n])
            bank = side_bank()
            for t in range(NT):
                s = nc.tensor.transpose(ps[0:HU, bank, t * P:t * P + P], maxes[:, w, :, t], k.ident[:, :])
            s = max_read[w] = pe.did(s)
            act.after(s, in_place[n - 2] if n >= 2 else None)
            s = side_read[bank] = act.did(nc.scalar.activation(max_t[:, w, :], ps[0:HU, bank, :], ACT.Copy, scale=-1.0))
            act.after(s, o2_last[n - 3] if n >= 3 else None)
            for g in range(HU):
                in_place[n] = max_dmas[w].start(act, q_stack[ROWS - 1:ROWS, n % 3, g, :].bitcast(F32),
                                                max_t[g:g + 1, w, :].bitcast(F32))

        def exponentials(n, tiles):
            w = n % 3
            pe.after(in_place[n])
            for t in range(NT):
                for g in range(HU):
                    o, e = n_o2[0] % len(O2_BANKS), n_o2[0] % N_EX
                    n_o2[0] += 1
                    bank = O2_BANKS[o]
                    pe.after(o2_read[o])
                    s = o2_last[n] = pe.did(nc.tensor.matmul(ps[:, bank, :], k_stack[:, w, g, t * P:t * P + P],
                                                             q_stack[:, w, g, :], start=True, stop=True))
                    act.after(s, ex_read[e], added[e])
                    s = o2_read[o] = act.did(nc.scalar.activation(ex[:, e, :], ps[:, bank, :], ACT.Exp, scale=SCALE))
                    tiles.append((e, s))
                    adder, engine = (dve, nc.vector) if n == UNITS - 1 else (pool, nc.gpsimd)
                    adder.after(s, ex_sum_read[0] if t == 1 else None)
                    if t > 0:
                        first = ex[:, tiles[g][0], :] if t == 1 else ex_sum[:, g, :]
                        adder.after(ex_sum_ready[g])
                        s = ex_sum_ready[g] = adder.did(engine.tensor_tensor(ex_sum[:, g, :], first, ex[:, e, :],
                                                                             ALU.add))
                        if t == 1:
                            added[tiles[g][0]] = s
                        added[e] = s
                    yield

        def weighted(n, tiles):
            b, c = n // (HB // HU), n % (HB // HU)
            pe.after(v_ready[b], sum_read[0])
            for t in range(NT):
                for g in range(HU):
                    e, ready = tiles[HU * t + g]
                    pe.after(ready)
                    at = P * c + 32 * g
                    s = nc.tensor.matmul(ps[32 * g:32 * g + 32, SUM_BANK, :], v[:, b % 2, t, at:at + 32], ex[:, e, :],
                                         start=t == 0, stop=t == NT - 1)
                s = pe.did(s)
                for g in range(HU):
                    ex_read[tiles[HU * t + g][0]] = s
                if t < NT - 1:
                    yield
            v_read[b] = s
            act.after(s, sums_free[0])
            sum_read[0] = act.did(nc.scalar.activation(sums_sb[:, 0, :], ps[:, SUM_BANK, :], ACT.Copy))
            ready = list(ex_sum_ready)

            def denominators():
                pe.after(*ready)
                bank = side_bank()
                for g in range(HU):
                    s = nc.tensor.matmul(ps[32 * g:32 * g + 32, bank, :], ones[:, :], ex_sum[:, g, :], start=True,
                                         stop=True)
                s = ex_sum_read[0] = pe.did(s)
                act.after(s)
                s = side_read[bank] = act.did(nc.scalar.activation(sums_sb[:, 1, :], ps[:, bank, :], ACT.Copy))
                divisions.extend(divide_steps(b, c, s))
                while n == UNITS - 1 and divisions:
                    divisions.pop(0)()
            side.insert(0, denominators)
            yield

        def divide_steps(b, c, ready):
            steps = []
            for piece in range(2 * NT):
                def go(piece=piece):
                    t, at = piece // 2, slice(piece * P // 2, piece * P // 2 + P // 2)
                    dve.after(ready, out_read[0])
                    s = dve.did(nc.vector.reciprocal(sums_sb[:, 1, at], sums_sb[:, 1, at]))
                    dve.after(s)
                    s = sums_free[0] = dve.did(nc.vector.tensor_tensor(out_t[:, c, at], sums_sb[:, 0, at],
                                                                       sums_sb[:, 1, at], ALU.mult))
                    if c == HB // HU - 1 and piece % 2:
                        side.append(project_step(b, t, s))
                steps.append(go)
            return steps

        def project_step(b, t, ready):
            def go():
                pe.after(ready, proj_weights.all())
                bank = side_bank()
                for c in range(ND):
                    s = nc.tensor.matmul(ps[:, bank, :], out_t[:, c, t * P:t * P + P], w_proj[:, c, :],
                                         start=c == 0, stop=c == ND - 1)
                    if c == ND // 2 - 1:
                        yield
                s = out_read[0] = pe.did(s)
                dve.after(s)
                side_read[bank] = dve.did(nc.vector.scalar_tensor_tensor(
                    x[:, NT * b + t, :], ps[:, bank, :], 1.0 - LAMBDA_INIT, x[:, NT * b + t, :], ALU.mult,
                    ALU.add))
                light.append(lambda ready=side_read[bank]: k.x_statistics(NT * b + t, ready))
            return go

        TILES, LAG = HU * NT, 6
        UNITS_B = HB // HU
        side, light, divisions = [], [], []
        due = []
        half_done = []

        def advance():
            step = half_done.pop() if half_done else side.pop(0)()
            if step and next(step, "done") is None:
                half_done.append(step)

        due = norm_steps(0)
        side += due[:ND]
        due = due[ND:]
        for step in light:
            step()
        light.clear()
        while side:
            advance()
        query_scale()
        side += query_key_steps(0)
        while side or half_done:
            advance()
        side, due = due, []
        while side or half_done:
            advance()
        proj_weights.start(sp, w_proj[:, :, :], d["wb_proj"])
        tiles = {}
        rows, own, sums = iter(()), iter(()), iter(())
        for m in range(TILES * (UNITS + 1) + LAG + HU + 4):
            n, i = m // TILES, m % TILES
            if i == 0 and n < UNITS:
                rows = maxima(n)
                if n % UNITS_B == 0 and n // UNITS_B + 1 < B:
                    due += norm_steps(n // UNITS_B + 1)
                share = (ND, 0, NT // 2, NT // 2)[n % UNITS_B]
                query_key = query_key_steps(n + 1) if n + 1 < UNITS else []
                side = query_key[:2] + side + due[:share]
                due = due[share:]
            if i == LAG + 1:
                side[:0] = query_key[2:]
                query_key = []
            if i == LAG and 1 <= n <= UNITS:
                tiles[n - 1] = []
                own = exponentials(n - 1, tiles[n - 1])
            if i == (LAG + HU) % TILES and 1 <= n <= UNITS:
                sums = weighted(n - 1, tiles[n - 1])
            next(own, None)
            if i == 2 and 1 <= n <= UNITS:
                place_maxima(n - 1)
            next(rows, None)
            if (i - LAG - HU) % HU == 0:
                next(sums, None)
            if side or half_done:
                advance()
            if divisions and (i % 2 or n % UNITS_B == 1):
                divisions.pop(0)()
            if light and (i % 2 == 0 or i < NT):
                light.pop(0)()
        while side or light or half_done:
            if light:
                light.pop(0)()
            else:
                advance()


def layout(inputs):
    import numpy as np

    def of(name):
        return np.asarray(inputs["L0_" + name])

    def feature_major(w):
        return w.T.reshape(ND, P, -1).transpose(1, 0, 2)

    a = {"x": of("attn_a_x")}
    a["gamma"] = of("attn_a_gamma").reshape(ND, P).T
    a["beta"] = of("attn_a_beta").reshape(ND, P).T
    a["w1_t"] = feature_major(of("attn_a_W1"))
    a["b1"] = of("attn_a_b1")[:, None]
    a["w2_t"] = of("attn_a_W2").T
    a["b2"] = of("attn_a_b2")[:, None]
    a["w3_t"] = of("attn_a_W3").T
    a["b3"] = of("attn_a_b3")
    a["wqkv_t"] = feature_major(of("attn_a_Wqkv"))
    a["b_qk"] = of("attn_a_bqkv")[:2 * KA, None]
    a["b_v"] = of("attn_a_bqkv")[2 * KA:]
    a["wout_t"] = of("attn_a_Wout").T
    a["bout"] = of("attn_a_bout")[None]
    one = np.eye(16, dtype=np.float32)
    a["own_head"] = np.concatenate([np.repeat(one, 2, axis=0)] * (HALVES // 2) + [one])

    oc, chunks = 2, NI // 2
    up = of("ffn_w_gate_up").reshape(2, chunks, oc, P, ND, P).transpose(1, 5, 4, 0, 2, 3).reshape(chunks, P, -1)
    down = of("ffn_w_down").T.reshape(chunks, oc, P, D).transpose(0, 2, 1, 3).reshape(chunks, P, -1)
    a["w_ffn"] = np.concatenate([up, down], axis=-1)

    w = of("attn_b_W_attn").reshape(ND, P, 3 * D).transpose(1, 0, 2)
    q1, k1, q2, k2 = (w[:, :, i * D // 2:(i + 1) * D // 2].reshape(P, ND, HB // 4, 4, HDB) for i in range(4))
    q = np.stack([q1, q2], axis=4).reshape(P, ND, HB // 4, P)
    k = np.stack([k1, k2], axis=4).reshape(P, ND, HB // 4, P)
    a["wb_qk"] = np.stack([q, k], axis=3)
    a["wb_v"] = w[:, :, 2 * D:]
    a["wb_proj"] = of("attn_b_W_proj").reshape(ND, P, D).transpose(1, 0, 2)
    a["lambdas"] = np.stack([of("attn_b_lambda_" + n) for n in ("q1", "k1", "q2", "k2")])[None]
    second = (np.arange(P) // HDB % 2).astype(np.float32)
    a["q2_row"] = second[None]
    a["q1_col"] = (np.arange(P) // HDB % 2 == 0).astype(np.float32)[:, None]
    return {name: np.ascontiguousarray(v) for name, v in a.items()}


def kernel(**inputs):
    import concourse.bacc as bacc
    from concourse.bass_utils import run_bass_kernel_spmd

    arrays = {"in_" + name: v for name, v in layout(inputs).items()}
    nc = bacc.Bacc("TRN2", target_bir_lowering=False, num_devices=1)
    d = {name[3:]: nc.dram_tensor(name, v.shape, mybir.dt.from_np(v.dtype), kind="ExternalInput").ap()
         for name, v in arrays.items()}
    d["out"] = nc.dram_tensor("out", (B, S, D), F32, kind="ExternalOutput").ap()
    build(nc, d)
    return run_bass_kernel_spmd(nc, [arrays], core_ids=[0]).results[0]["out"]
```
